# Optimizing a Trainium2 kernel written in Bass

```python
import numpy as np
import jax
import jax.numpy as jnp

def _softmax(x, axis=-1):
    return jax.nn.softmax(x, axis=axis)

def _gelu(x):
    return jax.nn.gelu(x, approximate=True)

def _silu(x):
    return jax.nn.silu(x)

def _sigmoid(x):
    return jax.nn.sigmoid(x)

def _layernorm(x, axis=-1, eps=1e-05):
    m = jnp.mean(x, axis=axis, keepdims=True)
    v = jnp.var(x, axis=axis, keepdims=True)
    return (x - m) / jnp.sqrt(v + eps)

def _scatter_add(tgt, idx, src, axis=0):
    return tgt.at[idx].add(src)

def _segment_sum(src, seg, n):
    return jax.ops.segment_sum(src, seg, n)
kernel_name = 'mk_cond_seq_d1_seqx_r4_0f0baf'

def setup_inputs(seed: int=0):
    np.random.seed(seed)
    _w = jnp.asarray

    def _rec_inputs():
        import jax
        import jax.numpy as jnp
        _rk = jax.random.key(seed)
        x = -0.0003482 + 1 * jax.random.normal(jax.random.fold_in(_rk, 1), (2, 1024, 288), jnp.float32)
        _lenS = 1024 - jax.random.randint(jax.random.fold_in(_rk, 7), (2,), 0, max(1, 1024 // 4) + 1, jnp.int32)
        _lenS2 = 1024 - jax.random.randint(jax.random.fold_in(_rk, 8), (2,), 0, max(1, 1024 // 4) + 1, jnp.int32)
        cond_1152 = -0.00342701 + 1.00097 * jax.random.normal(jax.random.fold_in(_rk, 11), (2, 288), jnp.float32)
        return (x, cond_1152)
    x, cond_1152 = _rec_inputs()

    def _L0_cond_setup():
        import jax, jax.numpy as jnp
        import numpy as np
        B, T, D, H = (64, 64, 288, 16)
        HD = D // H
        EPS = 1e-06

        def _ln(x):
            mu = jnp.mean(x, axis=-1, keepdims=True)
            var = jnp.var(x, axis=-1, keepdims=True)
            return (x - mu) * jax.lax.rsqrt(var + EPS)

        def _modulate(x, shift, scale):
            return x * (1.0 + scale[:, None, :]) + shift[:, None, :]

        def _attn(x, Wq, Wk, Wv, Wp, bp):
            b, t, d = x.shape
            q = (x @ Wq).reshape(b, t, H, HD).transpose(0, 2, 1, 3)
            k = (x @ Wk).reshape(b, t, H, HD).transpose(0, 2, 1, 3)
            v = (x @ Wv).reshape(b, t, H, HD).transpose(0, 2, 1, 3)
            scores = jnp.einsum('bhqd,bhkd->bhqk', q, k) / np.sqrt(HD)
            mask = jnp.triu(jnp.ones((t, t), bool), k=1)
            scores = jnp.where(mask, -jnp.inf, scores)
            w = jax.nn.softmax(scores, axis=-1)
            ctx = jnp.einsum('bhqk,bhkd->bhqd', w, v).transpose(0, 2, 1, 3).reshape(b, t, d)
            return ctx @ Wp + bp

        def _mlp(x, W1, b1, W2, b2):
            return jax.nn.silu(x @ W1 + b1) @ W2 + b2
        key = jax.random.key(seed)
        ks = jax.random.split(key, 12)
        s = lambda fan_in: 1.0 / np.sqrt(fan_in)
        return {'x': jax.random.normal(ks[0], (B, T, D), jnp.float32), 'c': jax.random.normal(ks[1], (B, D), jnp.float32), 'Wq': jax.random.normal(ks[2], (D, D), jnp.float32) * s(D), 'Wk': jax.random.normal(ks[3], (D, D), jnp.float32) * s(D), 'Wv': jax.random.normal(ks[4], (D, D), jnp.float32) * s(D), 'Wp': jax.random.normal(ks[5], (D, D), jnp.float32) * s(D), 'bp': jnp.zeros((D,), jnp.float32), 'W1': jax.random.normal(ks[6], (D, 4 * D), jnp.float32) * s(D), 'b1': jnp.zeros((4 * D,), jnp.float32), 'W2': jax.random.normal(ks[7], (4 * D, D), jnp.float32) * s(4 * D), 'b2': jnp.zeros((D,), jnp.float32), 'Wa': jax.random.normal(ks[8], (D, 6 * D), jnp.float32) * s(D), 'ba': jnp.zeros((6 * D,), jnp.float32)}
    _L0_cond_all = _L0_cond_setup()
    _L0_cond_in = {k: v for k, v in _L0_cond_all.items() if k in ('Wq', 'Wk', 'Wv', 'Wp', 'bp', 'W1', 'b1', 'W2', 'b2', 'Wa', 'ba')}
    del _L0_cond_all
    return {'x': x, 'cond_1152': cond_1152, 'L0_cond_Wq': _L0_cond_in['Wq'], 'L0_cond_Wk': _L0_cond_in['Wk'], 'L0_cond_Wv': _L0_cond_in['Wv'], 'L0_cond_Wp': _L0_cond_in['Wp'], 'L0_cond_bp': _L0_cond_in['bp'], 'L0_cond_W1': _L0_cond_in['W1'], 'L0_cond_b1': _L0_cond_in['b1'], 'L0_cond_W2': _L0_cond_in['W2'], 'L0_cond_b2': _L0_cond_in['b2'], 'L0_cond_Wa': _L0_cond_in['Wa'], 'L0_cond_ba': _L0_cond_in['ba']}

def reference(x, cond_1152, L0_cond_Wq, L0_cond_Wk, L0_cond_Wv, L0_cond_Wp, L0_cond_bp, L0_cond_W1, L0_cond_b1, L0_cond_W2, L0_cond_b2, L0_cond_Wa, L0_cond_ba):
    import jax
    import jax.numpy as jnp

    def _L0_cond_ref(x, c, Wq, Wk, Wv, Wp, bp, W1, b1, W2, b2, Wa, ba):
        import jax, jax.numpy as jnp
        import numpy as np
        B, T, D, H = (64, 64, 288, 16)
        HD = D // H
        EPS = 1e-06

        def _ln(x):
            mu = jnp.mean(x, axis=-1, keepdims=True)
            var = jnp.var(x, axis=-1, keepdims=True)
            return (x - mu) * jax.lax.rsqrt(var + EPS)

        def _modulate(x, shift, scale):
            return x * (1.0 + scale[:, None, :]) + shift[:, None, :]

        def _attn(x, Wq, Wk, Wv, Wp, bp):
            b, t, d = x.shape
            q = (x @ Wq).reshape(b, t, H, HD).transpose(0, 2, 1, 3)
            k = (x @ Wk).reshape(b, t, H, HD).transpose(0, 2, 1, 3)
            v = (x @ Wv).reshape(b, t, H, HD).transpose(0, 2, 1, 3)
            scores = jnp.einsum('bhqd,bhkd->bhqk', q, k) / np.sqrt(HD)
            mask = jnp.triu(jnp.ones((t, t), bool), k=1)
            scores = jnp.where(mask, -jnp.inf, scores)
            w = jax.nn.softmax(scores, axis=-1)
            ctx = jnp.einsum('bhqk,bhkd->bhqd', w, v).transpose(0, 2, 1, 3).reshape(b, t, d)
            return ctx @ Wp + bp

        def _mlp(x, W1, b1, W2, b2):
            return jax.nn.silu(x @ W1 + b1) @ W2 + b2
        mod = jax.nn.silu(c) @ Wa + ba
        sh_msa, sc_msa, g_msa, sh_mlp, sc_mlp, g_mlp = jnp.split(mod, 6, axis=1)
        x = x + g_msa[:, None, :] * _attn(_modulate(_ln(x), sh_msa, sc_msa), Wq, Wk, Wv, Wp, bp)
        x = x + g_mlp[:, None, :] * _mlp(_modulate(_ln(x), sh_mlp, sc_mlp), W1, b1, W2, b2)
        return x
    x = _L0_cond_ref(x, cond_1152, L0_cond_Wq, L0_cond_Wk, L0_cond_Wv, L0_cond_Wp, L0_cond_bp, L0_cond_W1, L0_cond_b1, L0_cond_W2, L0_cond_b2, L0_cond_Wa, L0_cond_ba)
    return x

_drawn_inputs = setup_inputs


def setup_inputs(seed=0):
    import zlib

    import numpy as np

    out = dict(_drawn_inputs(seed))
    spreads = {'L0_cond_bp': (0.0, 0.1),
     'L0_cond_b1': (0.0, 0.1),
     'L0_cond_b2': (0.0, 0.1),
     'L0_cond_ba': (0.0, 0.1)}
    factors = {}
    for name, (base, spread) in spreads.items():
        noise = np.random.default_rng([zlib.crc32(name.encode()), seed]).standard_normal(out[name].shape)
        drawn = base * np.exp(spread * noise) if base else spread * noise
        out[name] = jnp.asarray(drawn.astype(out[name].dtype))
    for name, factor in factors.items():
        out[name] = (out[name] * factor).astype(out[name].dtype)
    return out
```

```python
import numpy as np
import concourse.bass as bass
from concourse import mybir


def conditioned_transformer_block(nc, x, cond, Wq, Wk, Wv, Wp, bp, W1, b1, W2, b2, Wa, ba, out):
    f32, f32r, bf16, f16 = mybir.dt.float32, mybir.dt.float32r, mybir.dt.bfloat16, mybir.dt.float16
    ALU, ACT, AX = mybir.AluOpType, mybir.ActivationFunctionType, mybir.AxisListType

    B, L, D = x.shape
    P = nc.NUM_PARTITIONS
    H = 16
    HD = D // H
    F = W1.shape[1]
    EPS = 1e-6
    SCALE = 1.0 / float(np.sqrt(HD))
    NEG = -1e30
    TILES = B * L // P
    TQ = L // P
    CHUNK = 512
    CT = CHUNK // P
    FULL = D // P
    REM = D - FULL * P
    XC = D + 2 * REM
    RR = 3 * REM
    RB = RR + 2
    MF = F // P
    QKP = [P, P, P, P, 2 * D - 4 * P]
    QK_RUNS = [[(max(a, lo) - a, min(a + rows, hi) - max(a, lo), w, max(a, lo) - lo)
                for w, (lo, hi) in enumerate(((0, D), (D, 2 * D))) if max(a, lo) < min(a + rows, hi)]
               for a, rows in zip(range(0, 5 * P, P), QKP)]
    HEADS = B * H
    SR = 3 * HD
    SM = SR + 2
    VP = HD + 1
    KC = 96
    NK = D // KC

    GROUPS = [[0], [1, 7], [2, 6], [3, 5], [4]]
    GW = [sum(L - P * kt for kt in g) for g in GROUPS]
    GOFF = [sum(GW[:g]) for g in range(len(GROUPS))]
    NG = len(GROUPS)
    PCOLS = sum(GW)
    KOFF = {}
    for g, kts in enumerate(GROUPS):
        at = GOFF[g]
        for kt in kts:
            KOFF[kt] = at
            at += L - P * kt
    ORDER = [7, 3, 6, 2, 5, 1, 4, 0]
    VALUES_AT = [[0, 1, 2, 3, 4], [5, 6], [7], [], [], [], [], []]
    SCORES_T_AT = {2: 0, 3: 1, 4: 2, 5: 3, 6: 4}
    LO_VECTOR_AT, SUMS_AT = {1: 1, 3: 4}, 4
    WARM_AT = 3
    LOOPED = 6
    FIRST = HEADS % LOOPED + LOOPED
    GROUP_OF = {kt: g for g, kts in enumerate(GROUPS) for kt in kts}
    VECTOR_LOS, POOL_LOS = [1, 4], [0, 2, 3]

    qk_dram = nc.dram_tensor("qk_scratch", [2, 2, B * D, L], f32).ap()

    cursor = [nc.sbuf_base + 63 & ~63]

    def place(name, shape, dt, at=None):
        size = int(np.prod(shape[1:])) * (2 if dt in (bf16, f16) else 4)
        where = cursor[0] if at is None else at[0]
        t = nc.alloc_sbuf_tensor_at(name, shape, dt, offset=where)
        (cursor if at is None else at)[0] = where + (size + 31 & ~31)
        return t

    x_sb = place("x_sb", [P, TILES, D], f32)
    ctx_at = [cursor[0]]
    ctx_sb = place("ctx_sb", [P, TQ, B, D], f32)
    gate = place("gate", [P, B, 2, D], f32)
    modv = place("modv", [P, B, 3, 4], f32)
    mod_now = place("mod_now", [P, 3, 4], f32)
    stats = place("stats", [P, TILES, 6], f32)
    lnv = place("lnv", [P, 6, TILES], f32)
    pt3_at = [cursor[0]]
    xn = place("xn", [P, 2, CT, XC], f32)
    y = place("y", [P, 2, 3, CHUNK], f32)
    xh = place("xh", [P, 2, FULL, CHUNK], f32r)
    xl = place("xl", [P, 2, FULL, CHUNK], f32r)
    xr = place("xr", [P, 2, CHUNK], f32r)
    minus1 = place("minus1", [P, P], f32r)
    ident = place("ident", [P, P], f32)
    ident_b = place("ident_b", [P, P], bf16)
    mask = place("mask", [P, P], bf16)
    mask_t = place("mask_t", [P, P], bf16)
    wp_h = place("wp_h", [P, FULL, D], f32r)
    wp_l = place("wp_l", [P, FULL, D], f32r)
    wp_r = place("wp_r", [P, D], f32r)
    res = place("res", [P, 2, D], f32)
    area = cursor[0]

    a1 = [area]
    wqkv_h = place("wqkv_h", [P, FULL, 3 * D], f32r, a1)
    wqkv_l = place("wqkv_l", [P, FULL, 3 * D], f32r, a1)
    wqkv_r = place("wqkv_r", [P, 3 * D], f32r, a1)
    raw = place("raw", [P, 3, 4 * D], f32, a1)
    qk_st = place("qk_st", [P, 5, 2, CHUNK], f32r, a1)
    wa_sb = place("wa_sb", [P, NK, 6 * D], f32, a1)
    c_t = place("c_t", [P, NK, B], f32, a1)
    sc_t = place("sc_t", [P, NK, B], f32, a1)
    sc_b = place("sc_b", [P, NK, B, P], f32, a1)

    a2 = [area]
    pt = [place(f"pt{i}", [P, PCOLS], f32, a2 if i < 2 else pt3_at) for i in range(3)]
    pt_lo = [place(f"pt_lo{i}", [P, PCOLS], f16, a2 if i < 2 else pt3_at) for i in range(3)]
    q_st = place("q_st", [P, 2, L], f32r, a2)
    k_st = place("k_st", [P, 2, L], f32r, a2)
    mneg = place("mneg", [P, 3, P], f32, a2)
    m_t = place("m_t", [P, 3, 2, P], f32r, a2)
    csum = place("csum", [P, 3, TQ, VP], f32, a2)
    rden = place("rden", [P, 3, TQ], f32, a2)

    a3 = [area]
    h_h = place("h_h", [P, MF, CHUNK], f32r, a3)
    h_l = place("h_l", [P, MF, CHUNK], f32r, ctx_at)
    w1_h = place("w1_h", [P, FULL, F], f32r, a3)
    w1_l = place("w1_l", [P, FULL, F], f32r, a3)
    w1_r = place("w1_r", [P, F], f32r, a3)
    w2_h = place("w2_h", [P, MF, D], f32r, a3)
    w2_l = place("w2_l", [P, MF, D], f32r, a3)
    w2_r = place("w2_r", [P, D], f32r, a3)

    v_at = max(a1[0], a2[0], a3[0])
    av = [v_at]
    v_sb = place("v_sb", [P, HEADS, TQ, 3 * VP], bf16, av)
    v_res = place("v_res", [P, 2, D], f32, av)
    ar = [v_at]
    raw1 = place("raw1", [P, 3, F], f32, ar)
    raw2 = place("raw2", [P, MF, D], f32, ar)
    raw2b = place("raw2b", [P, D], f32, ar)
    hs = place("hs", [P, 3, CHUNK], f32, ar)
    assert max(av[0], ar[0]) <= nc.sbuf_usable_end, (av[0], ar[0], nc.sbuf_usable_end)

    from contextlib import ExitStack
    with ExitStack() as ctx:
        ps = ctx.enter_context(nc.psum_tensor("ps", [P, 8, 512], f32))

        def sem(name):
            return ctx.enter_context(nc.semaphore(name))

        x_in = [sem(f"x_in{c}") for c in range(B * L // CHUNK)]
        cond_in, wa_in, wqkv_in, wp_in, w1_in, w2_in = (sem(n) for n in (
            "cond_in", "wa_in", "wqkv_in", "wp_in", "w1_in", "w2_in"))
        pool_made, consts_made, silu_c, cond_rows, mod_mm, mod_ready, gate_mm, gate_ready = (sem(n) for n in (
            "pool_made", "consts_made", "silu_c", "cond_rows", "mod_mm", "mod_ready", "gate_mm", "gate_ready"))
        bias_split = sem("bias_split")
        wqkv_hi, wqkv_split, wp_hi, wp_split, w1_hi, w1_split, w2_hi, w2_split = (sem(n) for n in (
            "wqkv_hi", "wqkv_split", "wp_hi", "wp_split", "w1_hi", "w1_split", "w2_hi", "w2_split"))
        ln_step, std_ready, mod_copied, xn_ready, t_ready, y_ready, xh_ready, xl_ready, xt_used = (sem(n) for n in (
            "ln_step", "std_ready", "mod_copied", "xn_ready", "t_ready", "y_ready", "xh_ready", "xl_ready", "xt_used"))
        qk_ready, qk_hi, qk_evac, v_ready, v_hi, v_evac, v_mid, v_split = (sem(n) for n in (
            "qk_ready", "qk_hi", "qk_evac", "v_ready", "v_hi", "v_evac", "v_mid", "v_split"))
        qk_out = [sem(f"qk_out{m}") for m in range(5)]
        stacks_in = [sem(f"stacks_in{r}") for r in range(3)]
        m_rows = [sem(f"m_rows{r}") for r in range(3)]
        ones_ready, max_ready, max_used, mt_ready, mt_hi, mt_used, st_ready, exp_done = (sem(n) for n in (
            "ones_ready", "max_ready", "max_used", "mt_ready", "mt_hi", "mt_used", "st_ready", "exp_done"))
        lo_vector, lo_pool, pv_ready, pv_used, rden_ready, ctx_ready = (sem(n) for n in (
            "lo_vector", "lo_pool", "pv_ready", "pv_used", "rden_ready", "ctx_ready"))
        wp_ready, res1_ready, x2_ready, w1_ready, h_ready, hh_ready, hl_ready, w2_ready, res2_ready, x3_ready = (
            sem(n) for n in ("wp_ready", "res1_ready", "x2_ready", "w1_ready", "h_ready", "hh_ready", "hl_ready",
                             "w2_ready", "res2_ready", "x3_ready"))
        out_done = sem("out_done")

        block = ctx.enter_context(nc.Block())

        def count(v):
            return max(v, 0) if isinstance(v, int) else v

        x_tok = x.rearrange("b l d -> (b l) d")
        out_tok = out.rearrange("b l d -> (b l) d")
        slot2 = ps[:, 0:2, :].rearrange("p a c -> p (a c)")
        slot1 = ps[:, 2, :]
        st_slot = [ps[:, 3:5, :].rearrange("p a c -> p (a c)"), ps[:, 5:7, :].rearrange("p a c -> p (a c)")]
        pv = ps[:, 7, 0:TQ * 3 * VP].rearrange("p (i c) -> p i c", i=TQ)

        Y_CREDIT, XL_CREDIT, XT_CREDIT, V_CREDIT, VS_CREDIT = 3, 6, 2, CT, 2
        WP_CREDIT, RES_CREDIT, H_CREDIT, HS_CREDIT, W2_CREDIT = CT, 2, 3, 3, 2

        def v_part(j, par, t):
            return lambda i: v_sb[:, bass.ds(H * j, H), CT * par + t, i * VP:i * VP + HD]

        def lo_part(engine, n, r, g):
            cols = slice(GOFF[g], GOFF[g] + GW[g])
            w = pt[r][:, cols]
            return engine.tensor_tensor(pt_lo[r][:, cols], w, w.bitcast(bf16).rearrange("p (n e) -> p n e", e=2)[:, :, 1],
                                        ALU.subtract)

        def slot_of(i, g):
            return st_slot[(NG * i + g) % 2]

        wp_stage = raw[:, :, 3 * D:4 * D]

        def stack(tensor, r):
            return tensor[64 * (r % 2):64 * (r % 2) + SM, r // 2, :]

        def load_weight(eng, dst, src, signal):
            n = src.shape[1]
            eng.dma_start(dst[:, 0:FULL, 0:n], src[0:FULL * P, :].rearrange("(k p) n -> p k n", p=P)).then_inc(signal, 16)
            for i in range(3):
                eng.dma_start(dst[i * REM:(i + 1) * REM, FULL, 0:n], src[FULL * P:D, :]).then_inc(signal, 16)

        def load_bias(eng, dst, src, signal):
            for i in range(2):
                eng.dma_start(dst[i:i + 1, :], src.rearrange("(a n) -> a n", a=1)).then_inc(signal, 16)

        @block.sync
        def _(sp):
            for k in range(NK):
                with nc.allow_non_contiguous_dma(reason="the conditioning vector, a few hundred numbers"):
                    sp.dma_start(c_t[0:KC, k, :], cond[:, k * KC:(k + 1) * KC].rearrange("b p -> p b")).then_inc(cond_in, 16)
            for c in range(B * L // CHUNK):
                sp.dma_start(x_sb[:, c * CT:(c + 1) * CT, :],
                             x_tok[c * CHUNK:(c + 1) * CHUNK, :].rearrange("(t p) d -> p t d", p=P)).then_inc(x_in[c], 16)
            for i, w in enumerate((Wq, Wk, Wv)):
                load_weight(sp, raw[:, :, i * D:(i + 1) * D], w, wqkv_in)
            load_weight(sp, wp_stage, Wp, wp_in)
            load_bias(sp, wp_stage[RR:RB, FULL, :], bp, wp_in)

            with sp.Fori(0, B) as j:
                for par in range(2):
                    for m, rows in enumerate(QKP):
                        sp.wait_ge(qk_evac, 5 * (2 * j + par) + m + 1)
                        for at, n, which, col in QK_RUNS[m]:
                            sp.dma_start(qk_dram[:, which, bass.ds(D * j + col, n), par * CHUNK:(par + 1) * CHUNK].rearrange("e r c -> r e c"),
                                         qk_st[at:at + n, m, :, :].bitcast(f32)).then_inc(qk_out[m], 16)

            def load_stacks(n, r):
                q, k = stack(q_st, r).bitcast(f32), stack(k_st, r).bitcast(f32)
                for part, (qe, ke) in enumerate(((0, 0), (1, 0), (0, 1))):
                    to = slice(part * HD, (part + 1) * HD)
                    sp.dma_start(q[to, :], qk_dram[qe, 0, bass.ds(n * HD, HD), :]).then_inc(stacks_in[r], 16)
                    sp.dma_start(k[to, :], qk_dram[ke, 1, bass.ds(n * HD, HD), :]).then_inc(stacks_in[r], 16)

            def maximum_rows(n, r):
                sp.wait_ge(mt_used, n + 1)
                for e in range(2):
                    sp.dma_start(stack(q_st, r)[SR + e:SR + e + 1, :].bitcast(f32),
                                 m_t[0:TQ, r, e, :].bitcast(f32)).then_inc(m_rows[r], 16)

            for m in range(5):
                sp.wait_ge(qk_out[m], 16 * len(QK_RUNS[m]) * (B * L // CHUNK))
            sp.wait_ge(ones_ready, 1)
            load_stacks(0, 0)
            load_stacks(1, 1)

            def sp_head(n, r):
                if not isinstance(n, int) or 1 <= n <= HEADS:
                    maximum_rows(n - 1, (r - 1) % 3)
                if not isinstance(n, int) or 2 <= n and n + 1 < HEADS:
                    sp.wait_ge(st_ready, count(NG * (n - 1)))
                    load_stacks(n + 1, (r + 1) % 3)

            load_stacks(2, 2)
            for n in range(FIRST):
                sp_head(n, n % 3)
            with sp.Fori(0, (HEADS - FIRST) // LOOPED - 1) as j:
                for i in range(LOOPED):
                    sp_head(LOOPED * j + FIRST + i, (FIRST + i) % 3)
            for n in range(HEADS - LOOPED, HEADS + 1):
                sp_head(n, n % 3)

            sp.wait_ge(pv_ready, HEADS)
            load_weight(sp, raw1, W1, w1_in)
            load_bias(sp, raw1[RR:RB, FULL, :], b1, w1_in)
            sp.dma_start(raw2[:, :, :], W2.rearrange("(m p) n -> p m n", p=P)).then_inc(w2_in, 16)
            load_bias(sp, raw2b[RR:RB, :], b2, w2_in)

            with sp.Fori(0, B) as j:
                for par in range(2):
                    sp.wait_ge(x3_ready, CT * (2 * j + par + 1) + RES_CREDIT)
                    sp.dma_start(out_tok[bass.ds((2 * j + par) * CHUNK, CHUNK), :].rearrange("(t p) d -> p t d", p=P),
                                 x_sb[:, bass.ds((2 * j + par) * CT, CT), :]).then_inc(out_done, 16)
            sp.wait_ge(out_done, 16 * B * L // CHUNK)

        @block.gpsimd
        def _(pool):
            made = [0]

            def then_made(instruction):
                made[0] += 1
                instruction.then_inc(pool_made, 1)

            then_made(nc.gpsimd.memset(ident[:], 0.0))
            then_made(nc.gpsimd.memset(mask[:], 0.0))
            then_made(nc.gpsimd.memset(mask_t[:], 0.0))
            pool.wait_ge(pool_made, 3)
            then_made(nc.gpsimd.affine_select(out=ident[:], in_=ident[:], compare_op=ALU.not_equal, fill=1.0,
                                              base=0, pattern=[[-1, P]], channel_multiplier=1))
            then_made(nc.gpsimd.affine_select(out=mask[:], in_=mask[:], compare_op=ALU.is_ge, fill=NEG,
                                              base=0, pattern=[[-1, P]], channel_multiplier=1))
            then_made(nc.gpsimd.affine_select(out=mask_t[:], in_=mask_t[:], compare_op=ALU.is_ge, fill=NEG,
                                              base=0, pattern=[[1, P]], channel_multiplier=-1))
            pool.wait_ge(pool_made, 6)
            nc.gpsimd.tensor_copy(ident_b[:], ident[:]).then_inc(consts_made, 1)
            pool.dma_start(wa_sb[0:KC, :, :], Wa.rearrange("(k p) n -> p k n", p=KC)).then_inc(wa_in, 16)
            pool.dma_start(wa_sb[KC:KC + 1, 0, :], ba.rearrange("(a n) -> a n", a=1)).then_inc(wa_in, 16)

            def split_weight(hi_done, split, dst_h, dst_l, dst_r, src, n):
                pool.wait_ge(hi_done, 2)
                for k in range(FULL):
                    nc.gpsimd.tensor_tensor(dst_l[:, k, :], src[:, k, 0:n], dst_h[:, k, :].bitcast(f32), ALU.subtract).then_inc(split, 1)
                pool.wait_ge(split, FULL)
                nc.gpsimd.tensor_tensor(dst_r[REM:2 * REM, :], src[REM:2 * REM, FULL, 0:n],
                                        dst_r[REM:2 * REM, :].bitcast(f32), ALU.subtract).then_inc(split, 1)
                pool.wait_ge(split, FULL + 1)

            def lo_of_transposed(cc, par):
                for k in range(3):
                    pool.wait_ge(xh_ready, 3 * cc + k + 1)
                    if k < FULL:
                        nc.gpsimd.tensor_tensor(xl[:, par, k, :], y[:, par, k, :], xh[:, par, k, :].bitcast(f32),
                                                ALU.subtract).then_inc(xl_ready, 1)
                    else:
                        rows = slice(2 * REM, RR)
                        pool.wait_ge(xl_ready, 3 * cc + k + XL_CREDIT)
                        nc.gpsimd.tensor_tensor(xr[rows, par, :], y[rows, par, k, :], xr[rows, par, :].bitcast(f32),
                                                ALU.subtract).then_inc(xl_ready, 1)
                pool.wait_ge(xl_ready, 3 * (cc + 1) + XL_CREDIT)

            split_weight(wqkv_hi, wqkv_split, wqkv_h, wqkv_l, wqkv_r, raw, 3 * D)
            with pool.Fori(0, B) as j:
                for par in range(2):
                    lo_of_transposed(2 * j + par, par)
                for par in range(2):
                    for t in range(CT):
                        n = CT * (2 * j + par) + t
                        dst = v_part(j, par, t)
                        pool.wait_ge(v_evac, n + 1 + V_CREDIT)
                        nc.gpsimd.tensor_copy(dst(1), v_res[:, t % 2, :].rearrange("p (h d) -> p h d", h=H)).then_inc(v_mid, 1)
                        pool.wait_ge(v_mid, n + 1)
                        nc.gpsimd.tensor_tensor(dst(2), v_res[:, t % 2, :].rearrange("p (h d) -> p h d", h=H), dst(1),
                                                ALU.subtract).then_inc(v_split, 1)
            split_weight(wp_hi, wp_split, wp_h, wp_l, wp_r, wp_stage, D)

            def pool_lo(n, r, g):
                pool.wait_ge(exp_done, NG * n + g + 1)
                lo_part(nc.gpsimd, n, r, g).then_inc(lo_pool, 1)

            def pool_head(n, r):
                if not isinstance(n, int) or 2 <= n <= HEADS + 1:
                    pool_lo(n - 2, (r - 2) % 3, 3)
                if not isinstance(n, int) or 1 <= n <= HEADS:
                    pool_lo(n - 1, (r - 1) % 3, 0)
                if not isinstance(n, int) or 3 <= n <= HEADS + 2:
                    m = n - 3
                    pool.wait_ge(rden_ready, m + 1)
                    nc.gpsimd.tensor_tensor(
                        ctx_sb[:, :, :, :].rearrange("p i b d -> p i (b d)")[:, :, bass.ds(m * HD, HD)],
                        csum[:, r, :, 0:HD], rden[:, r, :].unsqueeze(2).to_broadcast([P, TQ, HD]), ALU.mult).then_inc(ctx_ready, 1)
                if not isinstance(n, int) or 1 <= n <= HEADS:
                    pool_lo(n - 1, (r - 1) % 3, 2)

            for n in range(FIRST):
                pool_head(n, n % 3)
            with pool.Fori(0, (HEADS - FIRST) // LOOPED) as j:
                for i in range(LOOPED):
                    pool_head(LOOPED * j + FIRST + i, (FIRST + i) % 3)
            for n in range(HEADS, HEADS + 3):
                pool_head(n, n % 3)

            with pool.Fori(0, B) as j:
                for par in range(2):
                    lo_of_transposed(4 + 2 * j + par, par)
                for par in range(2):
                    for t in range(CT):
                        pool.wait_ge(res1_ready, CT * (2 * j + par) + t + 1 + WP_CREDIT)
                        xt = x_sb[:, bass.ds(TQ * j + CT * par + t, 1), :]
                        nc.gpsimd.tensor_tensor(xt, xt, res[:, t % 2:t % 2 + 1, :], ALU.add).then_inc(x2_ready, 1)
            split_weight(w1_hi, w1_split, w1_h, w1_l, w1_r, raw1, F)
            pool.wait_ge(w2_hi, 1)
            nc.gpsimd.tensor_tensor(w2_l[:, :, :], raw2[:, :, :], w2_h[:, :, :].bitcast(f32), ALU.subtract).then_inc(w2_split, 1)

            with pool.Fori(0, B) as j:
                for par in range(2):
                    lo_of_transposed(8 + 2 * j + par, par)
                for par in range(2):
                    c = 2 * j + par
                    for m in range(MF):
                        pool.wait_ge(hh_ready, MF * c + m + 1)
                        nc.gpsimd.tensor_tensor(h_l[:, m, :], hs[:, m % 3, :], h_h[:, m, :].bitcast(f32),
                                                ALU.subtract).then_inc(hl_ready, 1)
                    for t in range(CT):
                        pool.wait_ge(res2_ready, CT * c + t + 1 + W2_CREDIT)
                        xt = x_sb[:, bass.ds(TQ * j + CT * par + t, 1), :]
                        nc.gpsimd.tensor_tensor(xt, xt, res[:, t % 2:t % 2 + 1, :], ALU.add).then_inc(x3_ready, 1)

        @block.scalar
        def _(act):
            act.wait_ge(cond_in, 16 * NK)
            act.wait_ge(cond_rows, 1)
            nc.scalar.activation(sc_t[0:KC, :, :], c_t[0:KC, :, :], ACT.Silu).then_inc(silu_c, 1)

            def round_weight(loaded, value, hi_done, dst_h, dst_r, src, n, rows):
                act.wait_ge(loaded, value)
                nc.scalar.activation(dst_h[:, :, :], src[:, 0:FULL, 0:n], ACT.Copy).then_inc(hi_done, 1)
                nc.scalar.activation(dst_r[0:rows, :], src[0:rows, FULL, 0:n], ACT.Copy).then_inc(hi_done, 1)

            def standard_deviation(value):
                act.wait_ge(ln_step, value)
                nc.scalar.activation(lnv[:, 4, :], lnv[:, 3, :], ACT.Sqrt).then_inc(std_ready, 1)

            def hi_of_transposed(cc, par):
                act.wait_ge(xt_used, cc - 2 + 1 + XT_CREDIT)
                for k in range(3):
                    act.wait_ge(y_ready, 3 * cc + k + 1 + Y_CREDIT)
                    if k < FULL:
                        nc.scalar.activation(xh[:, par, k, :], y[:, par, k, :], ACT.Copy).then_inc(xh_ready, 1)
                    else:
                        nc.scalar.activation(xr[0:RR, par, :], y[0:RR, par, k, :], ACT.Copy).then_inc(xh_ready, 1)

            round_weight(wqkv_in, 12 * 16, wqkv_hi, wqkv_h, wqkv_r, raw, 3 * D, RR)
            standard_deviation(TILES + 7)
            with act.Fori(0, B) as j:
                for par in range(2):
                    hi_of_transposed(2 * j + par, par)
                for par in range(2):
                    c = 2 * j + par
                    for m, rows in enumerate(QKP):
                        act.wait_ge(qk_out[m], 16 * len(QK_RUNS[m]) * c)
                        act.wait_ge(qk_ready, 5 * c + m + 1)
                        nc.scalar.activation(qk_st[0:rows, m, 0, :], ps[0:rows, 3 + m, :], ACT.Copy).then_inc(qk_hi, 1)
                    for t in range(CT):
                        act.wait_ge(v_ready, CT * c + t + 1)
                        nc.scalar.activation(v_part(j, par, t)(0), ps[:, 3 + t, 0:D].rearrange("p (h d) -> p h d", h=H),
                                             ACT.Copy).then_inc(v_hi, 1)
            round_weight(wp_in, 6 * 16, wp_hi, wp_h, wp_r, wp_stage, D, RB)

            def act_head(n, r, i):
                if isinstance(n, int) and not 1 <= n <= HEADS:
                    return
                m = n - 1
                act.wait_ge(pv_ready, count(m - 2))
                for g in range(NG):
                    act.wait_ge(st_ready, NG * m + g + 1)
                    nc.scalar.activation(pt[(r - 1) % 3][:, GOFF[g]:GOFF[g] + GW[g]],
                                         slot_of(i - 1, g)[:, 0:GW[g]], ACT.Exp, scale=SCALE).then_inc(exp_done, 1)

            for n in range(FIRST):
                act_head(n, n % 3, n)
            with act.Fori(0, (HEADS - FIRST) // LOOPED) as j:
                for i in range(LOOPED):
                    act_head(LOOPED * j + FIRST + i, (FIRST + i) % 3, FIRST + i)
            act_head(HEADS, HEADS % 3, HEADS)

            with act.Fori(0, B) as j:
                for par in range(2):
                    for t in range(CT):
                        act.wait_ge(ctx_ready, HEADS)
                        row = ctx_sb[:, CT * par + t, bass.ds(j, 1), :]
                        nc.scalar.activation(xn[:, par, t:t + 1, 0:D], row, ACT.Copy).then_inc(xn_ready, 1)
                        nc.scalar.activation(xn[:, par, t, D:XC].rearrange("p (e c) -> p e c", e=2),
                                             row[:, :, FULL * P:D].to_broadcast([P, 2, REM]), ACT.Copy).then_inc(xn_ready, 1)
                for par in range(2):
                    hi_of_transposed(4 + 2 * j + par, par)
            round_weight(w1_in, 6 * 16, w1_hi, w1_h, w1_r, raw1, F, RB)
            act.wait_ge(w2_in, 3 * 16)
            nc.scalar.activation(w2_h[:, :, :], raw2[:, :, :], ACT.Copy).then_inc(w2_hi, 1)
            nc.scalar.activation(w2_r[RR:RB, :], raw2b[RR:RB, :], ACT.Copy).then_inc(w2_hi, 1)
            standard_deviation(TILES + 8 + TILES + 7)
            with act.Fori(0, B) as j:
                for par in range(2):
                    hi_of_transposed(8 + 2 * j + par, par)
                for par in range(2):
                    c = 2 * j + par
                    for m in range(MF):
                        act.wait_ge(w1_ready, MF * c + m + 1)
                        act.wait_ge(hl_ready, MF * c + m - 3 + 1 + HS_CREDIT)
                        nc.scalar.activation(hs[:, m % 3, :], ps[:, 3 + m % 3, :], ACT.Silu).then_inc(h_ready, 1)

        @block.vector
        def _(dve):
            for signal, credit in ((y_ready, Y_CREDIT), (xl_ready, XL_CREDIT), (xt_used, XT_CREDIT), (v_evac, V_CREDIT),
                                   (v_split, VS_CREDIT), (res1_ready, WP_CREDIT), (x2_ready, RES_CREDIT),
                                   (x3_ready, RES_CREDIT), (h_ready, H_CREDIT), (hl_ready, HS_CREDIT), (res2_ready, W2_CREDIT)):
                dve.sem_inc(signal, credit)
            nc.vector.memset(sc_t[:], 1.0).then_inc(cond_rows, 1)
            nc.vector.memset(minus1[:].bitcast(f32), -1.0)
            nc.vector.memset(xr[RR:RB, :, :].bitcast(f32), -1.0).then_inc(cond_rows, 1)

            def statistics(tiles_ready, done):
                for t in range(TILES):
                    tiles_ready(t)
                    nc.vector.bn_stats(stats[:, t, :], x_sb[:, t, :]).then_inc(ln_step, 1)
                dve.wait_ge(ln_step, done + TILES)
                tt = nc.vector.tensor_tensor
                tt(lnv[:, 0, :], stats[:, :, 1], stats[:, :, 4], ALU.add).then_inc(ln_step, 1)
                tt(lnv[:, 1, :], stats[:, :, 1], stats[:, :, 4], ALU.subtract).then_inc(ln_step, 1)
                tt(lnv[:, 2, :], stats[:, :, 2], stats[:, :, 5], ALU.add).then_inc(ln_step, 1)
                dve.wait_ge(ln_step, done + TILES + 3)
                nc.vector.tensor_scalar(lnv[:, 0, :], lnv[:, 0, :], 0.5, None, ALU.mult).then_inc(ln_step, 1)
                tt(lnv[:, 1, :], lnv[:, 1, :], lnv[:, 1, :], ALU.mult).then_inc(ln_step, 1)
                nc.vector.tensor_scalar(lnv[:, 2, :], lnv[:, 2, :], 1.0 / D, EPS, ALU.mult, ALU.add).then_inc(ln_step, 1)
                dve.wait_ge(ln_step, done + TILES + 6)
                nc.vector.scalar_tensor_tensor(lnv[:, 3, :], lnv[:, 1, :], 0.25, lnv[:, 2, :], ALU.mult, ALU.add).then_inc(ln_step, 1)
                dve.wait_ge(std_ready, done // TILES + 1)
                nc.vector.reciprocal(lnv[:, 5, :], lnv[:, 4, :]).then_inc(ln_step, 1)
                dve.wait_ge(ln_step, done + TILES + 8)

            def normalized_rows(j, par):
                for t in range(CT):
                    tile = TQ * j + CT * par + t
                    mean, rstd = lnv[:, 0, bass.ds(tile, 1)], lnv[:, 5, bass.ds(tile, 1)]
                    nc.vector.tensor_scalar(xn[:, par, t:t + 1, 0:D], x_sb[:, bass.ds(tile, 1), :], mean, rstd,
                                            ALU.subtract, ALU.mult).then_inc(xn_ready, 1)
                    nc.vector.tensor_scalar(xn[:, par, t, D:XC].rearrange("p (e c) -> p e c", e=2),
                                            x_sb[:, bass.ds(tile, 1), FULL * P:D].to_broadcast([P, 2, REM]), mean, rstd,
                                            ALU.subtract, ALU.mult).then_inc(xn_ready, 1)

            def transposed(cc, par, kind):
                for k in range(3):
                    rows = slice(0, P) if k < FULL else slice(0, RR)
                    dve.wait_ge(t_ready, 3 * cc + k + 1)
                    dve.wait_ge(xl_ready, 3 * (cc - 2) + k + 1 + XL_CREDIT)
                    if kind is None:
                        nc.vector.tensor_copy(y[rows, par, k, :], ps[rows, k, :]).then_inc(y_ready, 1)
                    else:
                        nc.vector.tensor_scalar(y[rows, par, k, :], ps[rows, k, :], mod_now[rows, k, kind + 1:kind + 2],
                                                mod_now[rows, k, kind:kind + 1], ALU.mult, ALU.add).then_inc(y_ready, 1)

            def modulation_of(j, value):
                nc.vector.tensor_copy(mod_now[:, 0:FULL, :], modv[:, bass.ds(j, 1), 0:FULL, :].rearrange("p a k g -> p (a k) g")).then_inc(mod_copied, 1)
                nc.vector.tensor_copy(mod_now[0:RR, FULL:3, :], modv[0:RR, bass.ds(j, 1), FULL:3, :].rearrange("p a k g -> p (a k) g")).then_inc(mod_copied, 1)
                dve.wait_ge(mod_copied, value)

            def bias_rows(hi_done, dst_r, src):
                dve.wait_ge(hi_done, 2)
                nc.vector.scalar_tensor_tensor(dst_r[RR:RB, :], dst_r[RR:RB, :].bitcast(f32), ident[RR:RB, RR + 1:RR + 2],
                                               src[RR:RB, ...], ALU.mult, ALU.subtract).then_inc(bias_split, 1)

            statistics(lambda t: dve.wait_ge(x_in[t // CT], 16), 0)
            dve.wait_ge(silu_c, 1)
            dve.wait_ge(cond_rows, 2)
            for k in range(NK):
                rows = KC + 1 if k == 0 else KC
                nc.vector.tensor_copy(sc_b[0:rows, k, :, :], sc_t[0:rows, k, :].unsqueeze(2).to_broadcast([rows, B, P])).then_inc(silu_c, 1)
            dve.wait_ge(mod_mm, 1)
            mod_ps = ps[:, 0, 0:12 * B].rearrange("p (k g b) -> p k g b", k=3, g=4)
            for b in range(B):
                for rows, ks in ((slice(0, P), slice(0, FULL)), (slice(0, RR), slice(FULL, 3))):
                    nc.vector.tensor_copy(modv[rows, b, ks, 0::2], mod_ps[rows, ks, 0::2, b]).then_inc(mod_ready, 1)
                    nc.vector.tensor_scalar(modv[rows, b, ks, 1::2], mod_ps[rows, ks, 1::2, b], 1.0, None, ALU.add).then_inc(mod_ready, 1)
            dve.wait_ge(mod_ready, 8)
            dve.wait_ge(consts_made, 1)
            nc.vector.memset(v_sb[:, :, :, HD:HD + 1], 1.0)
            for i in (1, 2):
                last = nc.vector.memset(v_sb[:, :, :, i * VP + HD:(i + 1) * VP], 0.0)
            last.then_inc(v_split, 1)

            with dve.Fori(0, B) as j:
                modulation_of(j, 2 * (j + 1))
                for par in range(2):
                    normalized_rows(j, par)
                for par in range(2):
                    transposed(2 * j + par, par, 0)
                for par in range(2):
                    c = 2 * j + par
                    for m, rows in enumerate(QKP):
                        dve.wait_ge(qk_hi, 5 * c + m + 1)
                        nc.vector.tensor_tensor(qk_st[0:rows, m, 1, :], ps[0:rows, 3 + m, :], qk_st[0:rows, m, 0, :].bitcast(f32),
                                                ALU.subtract).then_inc(qk_evac, 1)
                    for t in range(CT):
                        dve.wait_ge(v_hi, CT * c + t + 1)
                        dve.wait_ge(v_split, CT * c + t - 2 + 1 + VS_CREDIT + 1)
                        nc.vector.tensor_tensor(v_res[:, t % 2, :].rearrange("p (h d) -> p h d", h=H),
                                                ps[:, 3 + t, 0:D].rearrange("p (h d) -> p h d", h=H), v_part(j, par, t)(0),
                                                ALU.subtract).then_inc(v_evac, 1)
            dve.wait_ge(gate_mm, 1)
            for b in range(B):
                for i in range(2):
                    nc.vector.tensor_copy(gate[:, b, i, :], ps[:, 2 * b + i, 0:D]).then_inc(gate_ready, 1)
            bias_rows(wp_hi, wp_r, wp_stage[:, FULL, :])

            for m in range(5):
                dve.wait_ge(qk_out[m], 16 * len(QK_RUNS[m]) * (B * L // CHUNK))
            dve.wait_ge(wp_split, FULL + 1)
            dve.wait_ge(bias_split, 1)
            nc.vector.memset(mneg[:], 0.0)
            nc.vector.memset(q_st[:].bitcast(f32), 1.0)
            nc.vector.memset(k_st[:].bitcast(f32), 1.0).then_inc(ones_ready, 1)

            def split_maximum(n, r):
                dve.wait_ge(mt_ready, n + 1)
                nc.vector.tensor_copy(m_t[0:TQ, r, 0, :], slot1[0:TQ, 0:P]).then_inc(mt_hi, 1)
                dve.wait_ge(mt_hi, n + 1)
                nc.vector.tensor_tensor(m_t[0:TQ, r, 1, :], slot1[0:TQ, 0:P], m_t[0:TQ, r, 0, :].bitcast(f32),
                                        ALU.subtract).then_inc(mt_used, 1)

            def vector_lo(n, r, g):
                dve.wait_ge(exp_done, NG * n + g + 1)
                lo_part(nc.vector, n, r, g).then_inc(lo_vector, 1)

            def sums(n, r):
                dve.wait_ge(pv_ready, n + 1)
                dve.wait_ge(ctx_ready, count(n - 2))
                nc.vector.tensor_reduce(csum[:, r, :, :], pv.rearrange("p i (e d) -> p i d e", e=3), axis=AX.X,
                                        op=ALU.add).then_inc(pv_used, 1)
                dve.wait_ge(pv_used, n + 1)
                nc.vector.reciprocal(rden[:, r, :], csum[:, r, :, HD]).then_inc(rden_ready, 1)

            def dve_head(n, r):
                fixed = isinstance(n, int)
                for s, i in enumerate(ORDER):
                    if s == 0 and (not fixed or 1 <= n <= HEADS):
                        split_maximum(n - 1, (r - 1) % 3)
                    if not fixed or n < HEADS:
                        dve.wait_ge(max_ready, TQ * n + s + 1)
                        src = (slot2 if s % 2 == 0 else slot1)[:, 0:(i + 1) * P]
                        nc.vector.tensor_reduce(mneg[:, r, i:i + 1], src, axis=AX.X, op=ALU.max, negate=True).then_inc(max_used, 1)
                    if s in LO_VECTOR_AT and (not fixed or 2 <= n <= HEADS + 1):
                        vector_lo(n - 2, (r - 2) % 3, LO_VECTOR_AT[s])
                    if s == SUMS_AT and (not fixed or 3 <= n <= HEADS + 2):
                        sums(n - 3, r)

            for n in range(FIRST):
                dve_head(n, n % 3)
            with dve.Fori(0, (HEADS - FIRST) // LOOPED) as j:
                for i in range(LOOPED):
                    dve_head(LOOPED * j + FIRST + i, (FIRST + i) % 3)
            for n in range(HEADS, HEADS + 3):
                dve_head(n, n % 3)

            with dve.Fori(0, B) as j:
                for par in range(2):
                    transposed(4 + 2 * j + par, par, None)
                for par in range(2):
                    for t in range(CT):
                        n = CT * (2 * j + par) + t
                        dve.wait_ge(wp_ready, n + 1)
                        dve.wait_ge(x2_ready, n - 2 + 1 + RES_CREDIT)
                        nc.vector.tensor_tensor(res[:, t % 2:t % 2 + 1, :], ps[:, 3 + t:4 + t, 0:D],
                                                gate[:, bass.ds(j, 1), 0, :], ALU.mult).then_inc(res1_ready, 1)
            bias_rows(w1_hi, w1_r, raw1[:, FULL, :])
            dve.wait_ge(w2_hi, 2)
            bias_rows(w2_hi, w2_r, raw2b)
            statistics(lambda t: dve.wait_ge(x2_ready, t + 1 + RES_CREDIT), TILES + 8)

            with dve.Fori(0, B) as j:
                modulation_of(j, 2 * B + 2 * (j + 1))
                for par in range(2):
                    normalized_rows(j, par)
                for par in range(2):
                    transposed(8 + 2 * j + par, par, 2)
                for par in range(2):
                    c = 2 * j + par
                    dve.wait_ge(w2_ready, CT * c)
                    for m in range(MF):
                        dve.wait_ge(h_ready, MF * c + m + 1 + H_CREDIT)
                        nc.vector.tensor_copy(h_h[:, m, :], hs[:, m % 3, :]).then_inc(hh_ready, 1)
                    for t in range(CT):
                        n = CT * c + t
                        dve.wait_ge(w2_ready, n + 1)
                        dve.wait_ge(x3_ready, n - 2 + 1 + RES_CREDIT)
                        nc.vector.tensor_tensor(res[:, t % 2:t % 2 + 1, :], ps[:, 6 + t % 2:7 + t % 2, 0:D],
                                                gate[:, bass.ds(j, 1), 1, :], ALU.mult).then_inc(res2_ready, 1)

        @block.tensor
        def _(pe):
            mm = nc.tensor.matmul

            pe.wait_ge(wa_in, 32)
            pe.wait_ge(silu_c, 1)
            pe.wait_ge(cond_rows, 2)
            for k in range(3):
                for g, group in enumerate((0, 1, 3, 4)):
                    at = (k * 4 + g) * B
                    for p0, cols in ([(0, P)] if k < FULL else [(i * REM, REM) for i in range(3)]):
                        for kk in range(NK):
                            rows = KC + 1 if kk == 0 else KC
                            last = mm(ps[p0:p0 + cols, 0, at:at + B], wa_sb[0:rows, kk, group * D + k * P:group * D + k * P + cols],
                                      sc_t[0:rows, kk, :], start=kk == 0, stop=kk == NK - 1)
            last.then_inc(mod_mm, 1)

            def transposes(cc, par, kind_wait):
                pe.wait_ge(xn_ready, 2 * CT * (cc + 1))
                for k in range(3):
                    cols = slice(k * P, (k + 1) * P) if k < FULL else slice(FULL * P, XC)
                    rows = P if k < FULL else RR
                    pe.wait_ge(y_ready, 3 * (cc - 1) + k + 1 + Y_CREDIT)
                    for t in range(CT):
                        last = nc.tensor.transpose(ps[0:rows, k, t * P:(t + 1) * P], xn[:, par, t, cols], ident[:])
                    last.then_inc(t_ready, 1)

            def products(out_ap, terms):
                for i, (lhs, rhs) in enumerate(terms):
                    last = mm(out_ap, lhs, rhs, start=i == 0, stop=i == len(terms) - 1)
                return last

            def weights_first(out_ap, wh, wl, wr, cols, par, rows):
                return products(out_ap, [(w, a) for k in range(FULL) for w, a in (
                    (wh[:, k, cols], xh[:, par, k, :]), (wl[:, k, cols], xh[:, par, k, :]), (wh[:, k, cols], xl[:, par, k, :]))]
                    + [(wr[0:rows, cols], xr[0:rows, par, :])])

            def tokens_first(out_ap, wh, wl, wr, cols, par, t, rows):
                tok = slice(t * P, (t + 1) * P)
                return products(out_ap, [(a, w) for k in range(FULL) for a, w in (
                    (xh[:, par, k, tok], wh[:, k, cols]), (xh[:, par, k, tok], wl[:, k, cols]), (xl[:, par, k, tok], wh[:, k, cols]))]
                    + [(xr[0:rows, par, tok], wr[0:rows, cols])])

            pe.wait_ge(consts_made, 1)
            pe.wait_ge(mod_ready, 8)
            with pe.Fori(0, B) as j:
                for par in range(2):
                    transposes(2 * j + par, par, None)
                for par in range(2):
                    c = 2 * j + par
                    pe.wait_ge(wqkv_split, FULL + 1)
                    pe.wait_ge(xl_ready, 3 * (c + 1) + XL_CREDIT)
                    for m, rows in enumerate(QKP):
                        if m < CT:
                            pe.wait_ge(v_evac, CT * (c - 1) + m + 1 + V_CREDIT)
                        else:
                            pe.wait_ge(qk_evac, 5 * c)
                        weights_first(ps[:, 3 + m, :], wqkv_h, wqkv_l, wqkv_r, slice(m * P, (m + 1) * P), par, RR).then_inc(qk_ready, 1)
                    for t in range(CT):
                        pe.wait_ge(qk_evac, 5 * c + t + 1)
                        last = tokens_first(ps[:, 3 + t, 0:D], wqkv_h, wqkv_l, wqkv_r, slice(2 * D, 3 * D), par, t, RR)
                        last.then_inc(v_ready, 1)
                    pe.wait_ge(v_ready, CT * (c + 1))
                    pe.sem_inc(xt_used, 1)

            pe.wait_ge(silu_c, 1 + NK)
            pe.wait_ge(y_ready, 3 * 4 + Y_CREDIT)
            pe.wait_ge(v_evac, TILES + V_CREDIT)
            for b in range(B):
                for i, group in enumerate((2, 5)):
                    for kk in range(NK):
                        rows = KC + 1 if kk == 0 else KC
                        last = mm(ps[:, 2 * b + i, 0:D], sc_b[0:rows, kk, b, :], wa_sb[0:rows, kk, group * D:(group + 1) * D],
                                  start=kk == 0, stop=kk == NK - 1)
            last.then_inc(gate_mm, 1)

            pe.wait_ge(gate_ready, 4)
            pe.wait_ge(qk_evac, 20)
            pe.wait_ge(v_split, TILES + 1 + VS_CREDIT)

            def pe_head(n, r, k3, place_of):
                fixed = isinstance(n, int)
                q, k = stack(q_st, r), stack(k_st, r)
                if fixed and n == WARM_AT:
                    warm = v_sb[:, 0, :, :].rearrange("p k c -> p (k c)")
                    for _ in range(8):
                        mm(ps[:, 7, 0:TQ * 3 * VP], ident_b[:], warm, start=True, stop=True)
                scores, maxima = not fixed or n < HEADS, not fixed or 1 <= n <= HEADS
                values = not fixed or 3 <= n <= HEADS + 2
                for s, i in enumerate(ORDER):
                    if scores:
                        if s == 0:
                            pe.wait_ge(stacks_in[r], 6 * 16 * (k3 + 1))
                        pe.wait_ge(max_used, count(TQ * n + s - 1))
                        if s == 1:
                            pe.wait_ge(mt_used, n)
                        slot = slot2 if s % 2 == 0 else slot1
                        for c0 in range(0, (i + 1) * P, CHUNK):
                            c1 = min(c0 + CHUNK, (i + 1) * P)
                            mm(slot[:, c0:c1], q[0:SR, i * P:(i + 1) * P], k[0:SR, c0:c1], start=True, stop=c1 < (i + 1) * P)
                        mm(slot[:, i * P:(i + 1) * P], ident_b[:], mask[:], start=False, stop=True).then_inc(max_ready, 1)
                    if s == 0 and maxima:
                        pe.wait_ge(max_used, TQ * n)
                        nc.tensor.transpose(slot1[:, 0:P], mneg[:, (r - 1) % 3, :], ident[:]).then_inc(mt_ready, 1)
                    if values:
                        for tile in VALUES_AT[s]:
                            weighted_values(n - 3, r, tile)
                    if maxima and s in SCORES_T_AT:
                        transposed_scores(n - 1, (r - 1) % 3, k3 if r else k3 - 1, SCORES_T_AT[s], place_of - 1)

            def transposed_scores(n, r, k3, g, place_of):
                q, k = stack(q_st, r), stack(k_st, r)
                slot = slot_of(place_of, g)
                if g == 0:
                    pe.wait_ge(m_rows[r], 2 * 16 * (k3 + 1))
                pe.wait_ge(exp_done, count(NG * n + g - 1))
                for kt in GROUPS[g]:
                    at = KOFF[kt] - GOFF[g]
                    c0 = 0
                    while c0 < L - P * kt:
                        c1 = min((at + c0) // CHUNK * CHUNK + CHUNK - at, L - P * kt)
                        mm(slot[:, at + c0:at + c1], k[:, kt * P:(kt + 1) * P], q[:, kt * P + c0:kt * P + c1],
                           start=(at + c0) % CHUNK == 0, stop=c0 > 0, skip_group_check=True)
                        c0 = c1
                    last = mm(slot[:, at:at + P], ident_b[:], mask_t[:], start=False, stop=True, skip_group_check=True)
                last.then_inc(st_ready, 1)

            def weighted_values(n, r, i):
                if i == 0:
                    pe.wait_ge(pv_used, n)
                for signal, groups in ((lo_vector, VECTOR_LOS), (lo_pool, POOL_LOS)):
                    done = max([groups.index(GROUP_OF[kt]) + 1 for kt in range(i + 1) if GROUP_OF[kt] in groups], default=0)
                    if done:
                        pe.wait_ge(signal, len(groups) * n + done)
                for kt in range(i + 1):
                    cols = slice(KOFF[kt] + (i - kt) * P, KOFF[kt] + (i - kt + 1) * P)
                    v = v_sb[:, bass.ds(n, 1), kt, :]
                    hi = pt[r][:, cols].bitcast(bf16).rearrange("p (n e) -> p n e", e=2)[:, :, 1]
                    mm(pv[:, i:i + 1, :], hi, v, start=kt == 0, stop=False)
                    last = mm(pv[:, i:i + 1, :], pt_lo[r][:, cols], v, start=False, stop=kt == i)
                if i == TQ - 1:
                    last.then_inc(pv_ready, 1)

            for n in range(FIRST):
                pe_head(n, n % 3, n // 3, n)
            with pe.Fori(0, (HEADS - FIRST) // LOOPED) as j:
                for i in range(LOOPED):
                    pe_head(LOOPED * j + FIRST + i, (FIRST + i) % 3, LOOPED // 3 * j + (FIRST + i) // 3, FIRST + i)
            for n in range(HEADS, HEADS + 3):
                pe_head(n, n % 3, n // 3, n)

            pe.wait_ge(exp_done, NG * HEADS)
            pe.wait_ge(mt_used, HEADS)
            pe.wait_ge(wp_split, FULL + 1)
            pe.wait_ge(bias_split, 1)
            with pe.Fori(0, B) as j:
                for par in range(2):
                    transposes(4 + 2 * j + par, par, None)
                for par in range(2):
                    c = 2 * j + par
                    pe.wait_ge(xl_ready, 3 * (4 + c + 1) + XL_CREDIT)
                    for t in range(CT):
                        pe.wait_ge(res1_ready, CT * (c - 1) + t + 1 + WP_CREDIT)
                        last = tokens_first(ps[:, 3 + t, 0:D], wp_h, wp_l, wp_r, slice(0, D), par, t, RB)
                        last.then_inc(wp_ready, 1)
                    pe.wait_ge(wp_ready, CT * (c + 1))
                    pe.sem_inc(xt_used, 1)

            pe.wait_ge(res1_ready, TILES + WP_CREDIT)
            pe.wait_ge(pv_used, HEADS)
            pe.wait_ge(w1_split, FULL + 1)
            pe.wait_ge(w2_split, 1)
            pe.wait_ge(bias_split, 3)
            with pe.Fori(0, B) as j:
                for par in range(2):
                    transposes(8 + 2 * j + par, par, None)
                for par in range(2):
                    c = 2 * j + par
                    pe.wait_ge(xl_ready, 3 * (8 + c + 1) + XL_CREDIT)
                    for m in range(MF):
                        pe.wait_ge(h_ready, MF * c + m - 3 + 1 + H_CREDIT)
                        last = weights_first(ps[:, 3 + m % 3, :], w1_h, w1_l, w1_r, slice(m * P, (m + 1) * P), par, RB)
                        last.then_inc(w1_ready, 1)
                    pe.wait_ge(w1_ready, MF * (c + 1))
                    pe.sem_inc(xt_used, 1)
                    for t in range(CT):
                        n = CT * c + t
                        tok = slice(t * P, (t + 1) * P)
                        pe.wait_ge(res2_ready, n - 2 + 1 + W2_CREDIT)
                        pe.wait_ge(hl_ready, MF * (c + 1) + HS_CREDIT)
                        products(ps[:, 6 + t % 2, 0:D], [(a, w) for m in range(MF) for a, w in (
                            (h_h[:, m, tok], w2_h[:, m, :]), (h_h[:, m, tok], w2_l[:, m, :]), (h_l[:, m, tok], w2_h[:, m, :]))]
                            + [(minus1[RR:RB, :], w2_r[RR:RB, :])]).then_inc(w2_ready, 1)


_INPUTS = ["x", "cond_1152", "L0_cond_Wq", "L0_cond_Wk", "L0_cond_Wv", "L0_cond_Wp", "L0_cond_bp", "L0_cond_W1",
           "L0_cond_b1", "L0_cond_W2", "L0_cond_b2", "L0_cond_Wa", "L0_cond_ba"]


def kernel(**inputs):
    import concourse.bacc as bacc
    from concourse.bass_utils import run_bass_kernel_spmd

    nc = bacc.Bacc("TRN2", target_bir_lowering=False, num_devices=1)
    arrays, args = {}, []
    for name in _INPUTS:
        a = np.ascontiguousarray(inputs[name])
        arrays[f"in_{name}"] = a
        args.append(nc.dram_tensor(f"in_{name}", a.shape, mybir.dt.from_np(a.dtype), kind="ExternalInput").ap())
    out = nc.dram_tensor("out", arrays["in_x"].shape, mybir.dt.float32, kind="ExternalOutput").ap()
    conditioned_transformer_block(nc, *args, out)
    r = run_bass_kernel_spmd(nc, [arrays], core_ids=[0])
    return r.results[0]["out"]
```

```python
import numpy as np
import concourse.bass as bass
from concourse import mybir


def conditioned_transformer_block(nc, x, cond, Wq, Wk, Wv, Wp, bp, W1, b1, W2, b2, Wa, ba, out):
    f32, f32r, bf16, f16 = mybir.dt.float32, mybir.dt.float32r, mybir.dt.bfloat16, mybir.dt.float16
    ALU, ACT, AX = mybir.AluOpType, mybir.ActivationFunctionType, mybir.AxisListType

    B, L, D = x.shape
    P = nc.NUM_PARTITIONS
    H = 16
    HD = D // H
    F = W1.shape[1]
    EPS = 1e-6
    SCALE = 1.0 / float(np.sqrt(HD))
    NEG = -1e30
    TILES = B * L // P
    TQ = L // P
    CHUNK = 512
    CT = CHUNK // P
    FULL = D // P
    REM = D - FULL * P
    XC = D + 2 * REM
    RR = 3 * REM
    RB = RR + 2
    MF = F // P
    QKP = [P, P, P, P, 2 * D - 4 * P]
    QK_RUNS = [[(max(a, lo) - a, min(a + rows, hi) - max(a, lo), w, max(a, lo) - lo)
                for w, (lo, hi) in enumerate(((0, D), (D, 2 * D))) if max(a, lo) < min(a + rows, hi)]
               for a, rows in zip(range(0, 5 * P, P), QKP)]
    HEADS = B * H
    SR = 3 * HD
    SM = SR + 2
    VP = HD + 1
    KC = 96
    NK = D // KC

    GROUPS = [[0], [1, 7], [2, 6], [3, 5], [4]]
    GW = [sum(L - P * kt for kt in g) for g in GROUPS]
    GOFF = [sum(GW[:g]) for g in range(len(GROUPS))]
    NG = len(GROUPS)
    PCOLS = sum(GW)
    KOFF = {}
    for g, kts in enumerate(GROUPS):
        at = GOFF[g]
        for kt in kts:
            KOFF[kt] = at
            at += L - P * kt
    ORDER = [7, 3, 6, 2, 5, 1, 4, 0]
    VALUES_AT = [[0, 1, 2, 3, 4], [5, 6], [7], [], [], [], [], []]
    SCORES_T_AT = {2: 0, 3: 1, 4: 2, 5: 3, 6: 4}
    LO_VECTOR_AT, SUMS_AT = {1: 1, 3: 4}, 4
    WARM_AT = 3
    LN_STEPS = TQ + 8
    LOOPED = 6
    FIRST = HEADS % LOOPED + LOOPED
    GROUP_OF = {kt: g for g, kts in enumerate(GROUPS) for kt in kts}
    VECTOR_LOS, POOL_LOS = [1, 4], [0, 2, 3]

    qk_dram = nc.dram_tensor("qk_scratch", [2, 2, B * D, L], f32).ap()

    cursor = [nc.sbuf_base + 63 & ~63]

    def place(name, shape, dt, at=None):
        size = int(np.prod(shape[1:])) * (2 if dt in (bf16, f16) else 4)
        where = cursor[0] if at is None else at[0]
        t = nc.alloc_sbuf_tensor_at(name, shape, dt, offset=where)
        (cursor if at is None else at)[0] = where + (size + 31 & ~31)
        return t

    x_sb = place("x_sb", [P, TILES, D], f32)
    ctx_at = [cursor[0]]
    ctx_sb = place("ctx_sb", [P, TQ, B, D], f32)
    gate = place("gate", [P, B, 2, D], f32)
    modv = place("modv", [P, B, 3, 4], f32)
    mod_now = place("mod_now", [P, 3, 4], f32)
    stats = place("stats", [P, TILES, 6], f32)
    lnv = place("lnv", [P, 6, TILES], f32)
    pt3_at = [cursor[0]]
    xn = place("xn", [P, 2, CT, XC], f32)
    y = place("y", [P, 2, 3, CHUNK], f32)
    xh = place("xh", [P, 2, FULL, CHUNK], f32r)
    xl = place("xl", [P, 2, FULL, CHUNK], f32r)
    xr = place("xr", [P, 2, CHUNK], f32r)
    minus1 = place("minus1", [P, P], f32r)
    ident = place("ident", [P, P], f32)
    ident_b = place("ident_b", [P, P], bf16)
    mask = place("mask", [P, P], bf16)
    mask_t = place("mask_t", [P, P], bf16)
    wp_h = place("wp_h", [P, FULL, D], f32r)
    wp_l = place("wp_l", [P, FULL, D], f32r)
    wp_r = place("wp_r", [P, D], f32r)
    res = place("res", [P, 2, D], f32)
    area = cursor[0]

    a1 = [area]
    wqkv_h = place("wqkv_h", [P, FULL, 3 * D], f32r, a1)
    wqkv_l = place("wqkv_l", [P, FULL, 3 * D], f32r, a1)
    wqkv_r = place("wqkv_r", [P, 3 * D], f32r, a1)
    raw = place("raw", [P, 3, 4 * D], f32, a1)
    qk_st = place("qk_st", [P, 5, 2, CHUNK], f32r, a1)
    wa_sb = place("wa_sb", [P, NK, 6 * D], f32, a1)
    c_t = place("c_t", [P, NK, B], f32, a1)
    sc_t = place("sc_t", [P, NK, B], f32, a1)
    sc_b = place("sc_b", [P, NK, B, P], f32, a1)

    a2 = [area]
    q_st = place("q_st", [P, 2, L], f32r, a2)
    k_st = place("k_st", [P, 2, L], f32r, a2)
    mneg = place("mneg", [P, 3, P], f32, a2)
    m_t = place("m_t", [P, 3, 2, P], f32r, a2)
    csum = place("csum", [P, 3, TQ, VP], f32, a2)
    rden = place("rden", [P, 3, TQ], f32, a2)
    stacks_end = a2[0]
    pt = [place(f"pt{i}", [P, PCOLS], f32, a2 if i < 2 else pt3_at) for i in range(3)]
    pt_lo = [place(f"pt_lo{i}", [P, PCOLS], f16, a2 if i < 2 else pt3_at) for i in range(3)]

    a3 = [area]
    w1_h = place("w1_h", [P, FULL, F], f32r, a3)
    w1_r = place("w1_r", [P, F], f32r, a3)
    w2_r = place("w2_r", [P, D], f32r, a3)
    assert a3[0] <= area + 2 * 2 * L * 4
    a3 = [stacks_end]
    w1_l = place("w1_l", [P, FULL, F], f32r, a3)
    h_h = place("h_h", [P, MF, CHUNK], f32r, a3)
    h_l = place("h_l", [P, MF, CHUNK], f32r, ctx_at)
    w2_h = place("w2_h", [P, MF, D], f32r, a3)
    w2_l = place("w2_l", [P, MF, D], f32r, a3)

    v_at = max(a1[0], a2[0], a3[0])
    av = [v_at]
    v_sb = place("v_sb", [P, HEADS, TQ, 3 * VP], bf16, av)
    v_res = place("v_res", [P, 2, D], f32, av)
    ar = [v_at]
    raw1 = place("raw1", [P, 3, F], f32, ar)
    raw2 = place("raw2", [P, MF, D], f32, ar)
    raw2b = place("raw2b", [P, D], f32, ar)
    hs = place("hs", [P, 3, CHUNK], f32, ar)
    V_HEADS_1 = -(-3 * F * 4 // (TQ * 3 * VP * 2))
    V_HEADS_2 = -(-(3 * F + MF * D + D) * 4 // (TQ * 3 * VP * 2))
    assert V_HEADS_2 <= HEADS - 3
    assert max(av[0], ar[0]) <= nc.sbuf_usable_end, (av[0], ar[0], nc.sbuf_usable_end)

    from contextlib import ExitStack
    with ExitStack() as ctx:
        ps = ctx.enter_context(nc.psum_tensor("ps", [P, 8, 512], f32))

        def sem(name):
            return ctx.enter_context(nc.semaphore(name))

        x_in = [sem(f"x_in{c}") for c in range(B * L // CHUNK)]
        wa_rest_in = sem("wa_rest_in")
        cond_in, wa_in, wqkv_in, wp_in, w1_in, w2_in = (sem(n) for n in (
            "cond_in", "wa_in", "wqkv_in", "wp_in", "w1_in", "w2_in"))
        pool_made, consts_made, silu_c, cond_rows, mod_mm, mod_ready, gate_mm, gate_ready = (sem(n) for n in (
            "pool_made", "consts_made", "silu_c", "cond_rows", "mod_mm", "mod_ready", "gate_mm", "gate_ready"))
        bias_split, mod2_mm = sem("bias_split"), sem("mod2_mm")
        wqkv_hi, wqkv_split, wp_hi, wp_split, w1_hi, w1_split, w2_hi, w2_split = (sem(n) for n in (
            "wqkv_hi", "wqkv_split", "wp_hi", "wp_split", "w1_hi", "w1_split", "w2_hi", "w2_split"))
        ln_step, std_ready, mod_copied, xn_ready, t_ready, y_ready, xh_ready, xl_ready, xt_used = (sem(n) for n in (
            "ln_step", "std_ready", "mod_copied", "xn_ready", "t_ready", "y_ready", "xh_ready", "xl_ready", "xt_used"))
        qk_ready, qk_hi, qk_evac, v_ready, v_hi, v_evac, v_mid, v_split = (sem(n) for n in (
            "qk_ready", "qk_hi", "qk_evac", "v_ready", "v_hi", "v_evac", "v_mid", "v_split"))
        qk_out = [sem(f"qk_out{m}") for m in range(5)]
        stacks_in = [sem(f"stacks_in{r}") for r in range(3)]
        m_rows = [sem(f"m_rows{r}") for r in range(3)]
        ones_ready, max_ready, max_used, mt_ready, mt_hi, mt_used, st_ready, exp_done = (sem(n) for n in (
            "ones_ready", "max_ready", "max_used", "mt_ready", "mt_hi", "mt_used", "st_ready", "exp_done"))
        lo_vector, lo_pool, pv_ready, pv_used, rden_ready, ctx_ready = (sem(n) for n in (
            "lo_vector", "lo_pool", "pv_ready", "pv_used", "rden_ready", "ctx_ready"))
        wp_ready, res1_ready, x2_ready, w1_ready, h_ready, hh_ready, hl_ready, w2_ready, res2_ready, x3_ready = (
            sem(n) for n in ("wp_ready", "res1_ready", "x2_ready", "w1_ready", "h_ready", "hh_ready", "hl_ready",
                             "w2_ready", "res2_ready", "x3_ready"))
        out_done = sem("out_done")

        block = ctx.enter_context(nc.Block())

        def count(v):
            return max(v, 0) if isinstance(v, int) else v

        x_tok = x.rearrange("b l d -> (b l) d")
        out_tok = out.rearrange("b l d -> (b l) d")
        slot2 = ps[:, 0:2, :].rearrange("p a c -> p (a c)")
        slot1 = ps[:, 2, :]
        st_slot = [ps[:, 3:5, :].rearrange("p a c -> p (a c)"), ps[:, 5:7, :].rearrange("p a c -> p (a c)")]
        pv = ps[:, 7, 0:TQ * 3 * VP].rearrange("p (i c) -> p i c", i=TQ)

        Y_CREDIT, XL_CREDIT, XT_CREDIT, V_CREDIT, VS_CREDIT = 3, 6, 2, CT, 2
        WP_CREDIT, RES_CREDIT, H_CREDIT, HS_CREDIT, W2_CREDIT = CT, 2, 3, 3, 2

        MOD_BANK = 7
        mod_ps = ps[:, MOD_BANK, 0:12 * B].rearrange("p (k g b) -> p k g b", k=3, g=4)

        def v_part(j, par, t):
            return lambda i: v_sb[:, bass.ds(H * j, H), CT * par + t, i * VP:i * VP + HD]

        def lo_part(engine, n, r, g):
            cols = slice(GOFF[g], GOFF[g] + GW[g])
            w = pt[r][:, cols]
            return engine.tensor_tensor(pt_lo[r][:, cols], w, w.bitcast(bf16).rearrange("p (n e) -> p n e", e=2)[:, :, 1],
                                        ALU.subtract)

        def slot_of(i, g):
            return st_slot[(NG * i + g) % 2]

        wp_stage = raw[:, :, 3 * D:4 * D]

        def stack(tensor, r):
            return tensor[64 * (r % 2):64 * (r % 2) + SM, r // 2, :]

        def load_weight(eng, dst, src, signal):
            n = src.shape[1]
            eng.dma_start(dst[:, 0:FULL, 0:n], src[0:FULL * P, :].rearrange("(k p) n -> p k n", p=P)).then_inc(signal, 16)
            for i in range(3):
                eng.dma_start(dst[i * REM:(i + 1) * REM, FULL, 0:n], src[FULL * P:D, :]).then_inc(signal, 16)

        def load_bias(eng, dst, src, signal):
            for i in range(2):
                eng.dma_start(dst[i:i + 1, :], src.rearrange("(a n) -> a n", a=1)).then_inc(signal, 16)

        @block.sync
        def _(sp):
            for k in range(NK):
                with nc.allow_non_contiguous_dma(reason="the conditioning vector, a few hundred numbers"):
                    sp.dma_start(c_t[0:KC, k, :], cond[:, k * KC:(k + 1) * KC].rearrange("b p -> p b")).then_inc(cond_in, 16)

            def load_tokens(c):
                sp.dma_start(x_sb[:, c * CT:(c + 1) * CT, :],
                             x_tok[c * CHUNK:(c + 1) * CHUNK, :].rearrange("(t p) d -> p t d", p=P)).then_inc(x_in[c], 16)

            for c in range(TQ // CT):
                load_tokens(c)
            for i, w in enumerate((Wq, Wk, Wv)):
                load_weight(sp, raw[:, :, i * D:(i + 1) * D], w, wqkv_in)
            load_weight(sp, wp_stage, Wp, wp_in)
            load_bias(sp, wp_stage[RR:RB, FULL, :], bp, wp_in)
            for c in range(TQ // CT, TILES // CT):
                load_tokens(c)

            with sp.Fori(0, B) as j:
                for par in range(2):
                    for m, rows in enumerate(QKP):
                        sp.wait_ge(qk_evac, 5 * (2 * j + par) + m + 1)
                        for at, n, which, col in QK_RUNS[m]:
                            sp.dma_start(qk_dram[:, which, bass.ds(D * j + col, n), par * CHUNK:(par + 1) * CHUNK].rearrange("e r c -> r e c"),
                                         qk_st[at:at + n, m, :, :].bitcast(f32)).then_inc(qk_out[m], 16)

            def load_stacks(n, r):
                q, k = stack(q_st, r).bitcast(f32), stack(k_st, r).bitcast(f32)
                for part, (qe, ke) in enumerate(((0, 0), (1, 0), (0, 1))):
                    to = slice(part * HD, (part + 1) * HD)
                    sp.dma_start(q[to, :], qk_dram[qe, 0, bass.ds(n * HD, HD), :]).then_inc(stacks_in[r], 16)
                    sp.dma_start(k[to, :], qk_dram[ke, 1, bass.ds(n * HD, HD), :]).then_inc(stacks_in[r], 16)

            def maximum_rows(n, r):
                sp.wait_ge(mt_used, n + 1)
                for e in range(2):
                    sp.dma_start(stack(q_st, r)[SR + e:SR + e + 1, :].bitcast(f32),
                                 m_t[0:TQ, r, e, :].bitcast(f32)).then_inc(m_rows[r], 16)

            for m in range(5):
                sp.wait_ge(qk_out[m], 16 * len(QK_RUNS[m]) * (B * L // CHUNK))
            sp.wait_ge(ones_ready, 1)
            load_stacks(0, 0)
            load_stacks(1, 1)

            def sp_head(n, r):
                if not isinstance(n, int) or 1 <= n <= HEADS:
                    maximum_rows(n - 1, (r - 1) % 3)
                if not isinstance(n, int) or 2 <= n and n + 1 < HEADS:
                    sp.wait_ge(st_ready, count(NG * (n - 1)))
                    load_stacks(n + 1, (r + 1) % 3)

            load_stacks(2, 2)
            for n in range(FIRST):
                sp_head(n, n % 3)
            with sp.Fori(0, (HEADS - FIRST) // LOOPED - 1) as j:
                for i in range(LOOPED):
                    sp_head(LOOPED * j + FIRST + i, (FIRST + i) % 3)
            sp.wait_ge(pv_ready, V_HEADS_1)
            load_weight(sp, raw1, W1, w1_in)
            load_bias(sp, raw1[RR:RB, FULL, :], b1, w1_in)
            for n in range(HEADS - LOOPED, HEADS + 1):
                sp_head(n, n % 3)
            sp.wait_ge(pv_ready, V_HEADS_2)
            sp.dma_start(raw2[:, :, :], W2.rearrange("(m p) n -> p m n", p=P)).then_inc(w2_in, 16)
            load_bias(sp, raw2b[RR:RB, :], b2, w2_in)

            with sp.Fori(0, B) as j:
                for par in range(2):
                    sp.wait_ge(x3_ready, CT * (2 * j + par + 1) + RES_CREDIT)
                    sp.dma_start(out_tok[bass.ds((2 * j + par) * CHUNK, CHUNK), :].rearrange("(t p) d -> p t d", p=P),
                                 x_sb[:, bass.ds((2 * j + par) * CT, CT), :]).then_inc(out_done, 16)
            sp.wait_ge(out_done, 16 * B * L // CHUNK)

        @block.gpsimd
        def _(pool):
            made = [0]

            def then_made(instruction):
                made[0] += 1
                instruction.then_inc(pool_made, 1)

            then_made(nc.gpsimd.memset(ident[:], 0.0))
            then_made(nc.gpsimd.memset(mask[:], 0.0))
            then_made(nc.gpsimd.memset(mask_t[:], 0.0))
            pool.wait_ge(pool_made, 3)
            then_made(nc.gpsimd.affine_select(out=ident[:], in_=ident[:], compare_op=ALU.not_equal, fill=1.0,
                                              base=0, pattern=[[-1, P]], channel_multiplier=1))
            then_made(nc.gpsimd.affine_select(out=mask[:], in_=mask[:], compare_op=ALU.is_ge, fill=NEG,
                                              base=0, pattern=[[-1, P]], channel_multiplier=1))
            then_made(nc.gpsimd.affine_select(out=mask_t[:], in_=mask_t[:], compare_op=ALU.is_ge, fill=NEG,
                                              base=0, pattern=[[1, P]], channel_multiplier=-1))
            pool.wait_ge(pool_made, 6)
            nc.gpsimd.tensor_copy(ident_b[:], ident[:]).then_inc(consts_made, 1)
            pool.dma_start(wa_sb[0:KC, :, 2 * D:], Wa[:, 2 * D:].rearrange("(k p) n -> p k n", p=KC)).then_inc(wa_rest_in, 16)

            def split_weight(hi_done, split, dst_h, dst_l, dst_r, src, n):
                pool.wait_ge(hi_done, 2)
                for k in range(FULL):
                    nc.gpsimd.tensor_tensor(dst_l[:, k, :], src[:, k, 0:n], dst_h[:, k, :].bitcast(f32), ALU.subtract).then_inc(split, 1)
                pool.wait_ge(split, FULL)
                nc.gpsimd.tensor_tensor(dst_r[REM:2 * REM, :], src[REM:2 * REM, FULL, 0:n],
                                        dst_r[REM:2 * REM, :].bitcast(f32), ALU.subtract).then_inc(split, 1)
                pool.wait_ge(split, FULL + 1)

            def lo_of_transposed(cc, ci, par):
                for k in range(3):
                    pool.wait_ge(xh_ready, 3 * cc + k + 1)
                    if k < FULL:
                        nc.gpsimd.tensor_tensor(xl[:, par, k, :], y[:, par, k, :], xh[:, par, k, :].bitcast(f32),
                                                ALU.subtract).then_inc(xl_ready, 1)
                    else:
                        rows = slice(2 * REM, RR)
                        pool.wait_ge(xl_ready, 3 * ci + k + XL_CREDIT)
                        nc.gpsimd.tensor_tensor(xr[rows, par, :], y[rows, par, k, :], xr[rows, par, :].bitcast(f32),
                                                ALU.subtract).then_inc(xl_ready, 1)
                pool.wait_ge(xl_ready, 3 * (ci + 1) + XL_CREDIT)

            split_weight(wqkv_hi, wqkv_split, wqkv_h, wqkv_l, wqkv_r, raw, 3 * D)
            lo_of_transposed(0, 0, 0)
            split_weight(wp_hi, wp_split, wp_h, wp_l, wp_r, wp_stage, D)

            def pool_first(j, last):
                for par in range(2):
                    if par == 0 or not last:
                        lo_of_transposed(2 * j + par + 1, 2 * j + par + 1, 1 - par)
                    for t in range(CT):
                        n = CT * (2 * j + par) + t
                        dst = v_part(j, par, t)
                        pool.wait_ge(v_evac, n + 1 + V_CREDIT)
                        nc.gpsimd.tensor_copy(dst(1), v_res[:, t % 2, :].rearrange("p (h d) -> p h d", h=H)).then_inc(v_mid, 1)
                        pool.wait_ge(v_mid, n + 1)
                        nc.gpsimd.tensor_tensor(dst(2), v_res[:, t % 2, :].rearrange("p (h d) -> p h d", h=H), dst(1),
                                                ALU.subtract).then_inc(v_split, 1)

            with pool.Fori(0, B - 1) as j:
                pool_first(j, False)
            pool_first(B - 1, True)

            def pool_lo(n, r, g):
                pool.wait_ge(exp_done, NG * n + g + 1)
                lo_part(nc.gpsimd, n, r, g).then_inc(lo_pool, 1)

            def pool_head(n, r):
                if not isinstance(n, int) or 2 <= n <= HEADS + 1:
                    pool_lo(n - 2, (r - 2) % 3, 3)
                if not isinstance(n, int) or 1 <= n <= HEADS:
                    pool_lo(n - 1, (r - 1) % 3, 0)
                if not isinstance(n, int) or 3 <= n <= HEADS + 2:
                    m = n - 3
                    pool.wait_ge(rden_ready, m + 1)
                    nc.gpsimd.tensor_tensor(
                        ctx_sb[:, :, :, :].rearrange("p i b d -> p i (b d)")[:, :, bass.ds(m * HD, HD)],
                        csum[:, r, :, 0:HD], rden[:, r, :].unsqueeze(2).to_broadcast([P, TQ, HD]), ALU.mult).then_inc(ctx_ready, 1)
                if not isinstance(n, int) or 1 <= n <= HEADS:
                    pool_lo(n - 1, (r - 1) % 3, 2)

            for n in range(FIRST):
                pool_head(n, n % 3)
            with pool.Fori(0, (HEADS - FIRST) // LOOPED) as j:
                for i in range(LOOPED):
                    pool_head(LOOPED * j + FIRST + i, (FIRST + i) % 3)
            for n in range(HEADS, HEADS + 3):
                pool_head(n, n % 3)

            pool.wait_ge(w1_hi, 2)
            pool.wait_ge(pv_ready, HEADS - 1)
            for k in range(FULL):
                nc.gpsimd.tensor_tensor(w1_l[:, k, :], raw1[:, k, :], w1_h[:, k, :].bitcast(f32), ALU.subtract).then_inc(w1_split, 1)
            with pool.Fori(0, B) as j:
                for t in range(TQ):
                    pool.wait_ge(res1_ready, TQ * j + t + 1 + WP_CREDIT)
                    xt = x_sb[:, bass.ds(TQ * j + t, 1), :]
                    nc.gpsimd.tensor_tensor(xt, xt, res[:, t % 2:t % 2 + 1, :], ALU.add).then_inc(x2_ready, 1)
            pool.wait_ge(w2_hi, 1)
            nc.gpsimd.tensor_tensor(w2_l[:, :, :], raw2[:, :, :], w2_h[:, :, :].bitcast(f32), ALU.subtract).then_inc(w2_split, 1)

            lo_of_transposed(8, 4, 0)

            def pool_mlp(j, last):
                for par in range(2):
                    c = 2 * j + par
                    for m in range(MF):
                        pool.wait_ge(hh_ready, MF * c + m + 1)
                        nc.gpsimd.tensor_tensor(h_l[:, m, :], hs[:, m % 3, :], h_h[:, m, :].bitcast(f32),
                                                ALU.subtract).then_inc(hl_ready, 1)
                    if par == 0 or not last:
                        lo_of_transposed(8 + c + 1, 4 + c + 1, 1 - par)
                    for t in range(CT):
                        pool.wait_ge(res2_ready, CT * c + t + 1 + W2_CREDIT)
                        xt = x_sb[:, bass.ds(TQ * j + CT * par + t, 1), :]
                        nc.gpsimd.tensor_tensor(xt, xt, res[:, t % 2:t % 2 + 1, :], ALU.add).then_inc(x3_ready, 1)

            with pool.Fori(0, B - 1) as j:
                pool_mlp(j, False)
            pool_mlp(B - 1, True)

        @block.scalar
        def _(act):
            act.dma_start(wa_sb[0:KC, :, 0:2 * D], Wa[:, 0:2 * D].rearrange("(k p) n -> p k n", p=KC)).then_inc(wa_in, 16)
            act.dma_start(wa_sb[KC:KC + 1, 0, :], ba.rearrange("(a n) -> a n", a=1)).then_inc(wa_in, 16)
            act.wait_ge(cond_in, 16 * NK)
            act.wait_ge(cond_rows, 1)
            nc.scalar.activation(sc_t[0:KC, :, :], c_t[0:KC, :, :], ACT.Silu).then_inc(silu_c, 1)

            def round_weight(loaded, value, hi_done, dst_h, dst_r, src, n, rows):
                act.wait_ge(loaded, value)
                nc.scalar.activation(dst_h[:, :, :], src[:, 0:FULL, 0:n], ACT.Copy).then_inc(hi_done, 1)
                nc.scalar.activation(dst_r[0:rows, :], src[0:rows, FULL, 0:n], ACT.Copy).then_inc(hi_done, 1)

            def standard_deviation(g, j):
                act.wait_ge(ln_step, LN_STEPS * g + LN_STEPS - 1)
                rows = bass.ds(TQ * j, TQ)
                nc.scalar.activation(lnv[:, 4, rows], lnv[:, 3, rows], ACT.Sqrt).then_inc(std_ready, 1)

            def hi_of_transposed(cc, par, from_psum=False):
                act.wait_ge(xt_used, cc - 2 + 1 + XT_CREDIT)
                for k in range(3):
                    if from_psum:
                        act.wait_ge(t_ready, 3 * cc + k + 1)
                    else:
                        act.wait_ge(y_ready, 3 * cc + k + 1 + Y_CREDIT)
                    rows = slice(0, P) if k < FULL else slice(0, RR)
                    src = ps[rows, k, :] if from_psum else y[rows, par, k, :]
                    nc.scalar.activation(xh[:, par, k, :] if k < FULL else xr[rows, par, :], src, ACT.Copy).then_inc(xh_ready, 1)

            round_weight(wqkv_in, 12 * 16, wqkv_hi, wqkv_h, wqkv_r, raw, 3 * D, RR)
            round_weight(wp_in, 6 * 16, wp_hi, wp_h, wp_r, wp_stage, D, RB)
            standard_deviation(0, 0)
            hi_of_transposed(0, 0)

            def act_first(j, last):
                for par in range(2):
                    c = 2 * j + par
                    for m, rows in enumerate(QKP):
                        act.wait_ge(qk_out[m], 16 * len(QK_RUNS[m]) * c)
                        act.wait_ge(qk_ready, 5 * c + m + 1)
                        nc.scalar.activation(qk_st[0:rows, m, 0, :], ps[0:rows, 3 + m, :], ACT.Copy).then_inc(qk_hi, 1)
                    if par == 0 and not last:
                        standard_deviation(j + 1, j + 1)
                    if par == 0 or not last:
                        hi_of_transposed(c + 1, 1 - par)
                    for t in range(CT):
                        act.wait_ge(v_ready, CT * c + t + 1)
                        nc.scalar.activation(v_part(j, par, t)(0), ps[:, 3 + t, 0:D].rearrange("p (h d) -> p h d", h=H),
                                             ACT.Copy).then_inc(v_hi, 1)

            with act.Fori(0, B - 1) as j:
                act_first(j, False)
            act_first(B - 1, True)

            def act_head(n, r, i):
                if isinstance(n, int) and not 1 <= n <= HEADS:
                    return
                m = n - 1
                act.wait_ge(pv_ready, count(m - 2))
                for g in range(NG):
                    act.wait_ge(st_ready, NG * m + g + 1)
                    nc.scalar.activation(pt[(r - 1) % 3][:, GOFF[g]:GOFF[g] + GW[g]],
                                         slot_of(i - 1, g)[:, 0:GW[g]], ACT.Exp, scale=SCALE).then_inc(exp_done, 1)

            for n in range(FIRST):
                act_head(n, n % 3, n)
            with act.Fori(0, (HEADS - FIRST) // LOOPED) as j:
                for i in range(LOOPED):
                    act_head(LOOPED * j + FIRST + i, (FIRST + i) % 3, FIRST + i)
            act_head(HEADS, HEADS % 3, HEADS)

            def context_rows(j, par):
                for t in range(CT):
                    row = ctx_sb[:, CT * par + t, bass.ds(j, 1), :]
                    nc.scalar.activation(xn[:, par, t:t + 1, 0:D], row, ACT.Copy).then_inc(xn_ready, 1)
                    nc.scalar.activation(xn[:, par, t, D:XC].rearrange("p (e c) -> p e c", e=2),
                                         row[:, :, FULL * P:D].to_broadcast([P, 2, REM]), ACT.Copy).then_inc(xn_ready, 1)

            act.wait_ge(pv_ready, HEADS - 2)
            act.wait_ge(st_ready, NG * HEADS)
            for j in range(B):
                act.wait_ge(ctx_ready, H * (j + 1))
                act.wait_ge(t_ready, 3 * 2 * (B + j))
                for par in range(2):
                    context_rows(j, par)
                if j == 0:
                    round_weight(w1_in, 6 * 16, w1_hi, w1_h, w1_r, raw1, F, RB)
                for par in range(2):
                    hi_of_transposed(2 * B + 2 * j + par, par, from_psum=True)
            act.wait_ge(w2_in, 3 * 16)
            nc.scalar.activation(w2_h[:, :, :], raw2[:, :, :], ACT.Copy).then_inc(w2_hi, 1)
            nc.scalar.activation(w2_r[RR:RB, :], raw2b[RR:RB, :], ACT.Copy).then_inc(w2_hi, 1)
            standard_deviation(B, 0)
            hi_of_transposed(4 * B, 0)

            def act_mlp(j, last):
                for par in range(2):
                    c = 2 * j + par
                    for m in range(MF):
                        act.wait_ge(w1_ready, MF * c + m + 1)
                        act.wait_ge(hl_ready, MF * c + m - 3 + 1 + HS_CREDIT)
                        nc.scalar.activation(hs[:, m % 3, :], ps[:, 3 + m % 3, :], ACT.Silu).then_inc(h_ready, 1)
                    if par == 0 or not last:
                        hi_of_transposed(4 * B + c + 1, 1 - par)
                    if par == 0 and not last:
                        standard_deviation(B + j + 1, j + 1)

            with act.Fori(0, B - 1) as j:
                act_mlp(j, False)
            act_mlp(B - 1, True)

        @block.vector
        def _(dve):
            for signal, credit in ((y_ready, Y_CREDIT), (xl_ready, XL_CREDIT), (xt_used, XT_CREDIT), (v_evac, V_CREDIT),
                                   (v_split, VS_CREDIT), (res1_ready, WP_CREDIT), (x2_ready, RES_CREDIT),
                                   (x3_ready, RES_CREDIT), (h_ready, H_CREDIT), (hl_ready, HS_CREDIT), (res2_ready, W2_CREDIT)):
                dve.sem_inc(signal, credit)
            nc.vector.memset(sc_t[:], 1.0).then_inc(cond_rows, 1)
            nc.vector.memset(minus1[:].bitcast(f32), -1.0)
            nc.vector.memset(xr[RR:RB, :, :].bitcast(f32), -1.0).then_inc(cond_rows, 1)
            nc.vector.memset(v_sb[:, :, :, HD:HD + 1], 1.0)
            for i in (1, 2):
                last = nc.vector.memset(v_sb[:, :, :, i * VP + HD:(i + 1) * VP], 0.0)
            last.then_inc(v_split, 1)

            def tile_statistics(g, j, ready):
                for t in range(TQ):
                    ready(t)
                    nc.vector.bn_stats(stats[:, bass.ds(TQ * j + t, 1), :].rearrange("p a c -> p (a c)"),
                                       x_sb[:, bass.ds(TQ * j + t, 1), :].rearrange("p a c -> p (a c)")).then_inc(ln_step, 1)

            def variances(g, j):
                base = LN_STEPS * g + TQ
                dve.wait_ge(ln_step, base)
                rows = bass.ds(TQ * j, TQ)
                tt = nc.vector.tensor_tensor
                tt(lnv[:, 0, rows], stats[:, rows, 1], stats[:, rows, 4], ALU.add).then_inc(ln_step, 1)
                tt(lnv[:, 1, rows], stats[:, rows, 1], stats[:, rows, 4], ALU.subtract).then_inc(ln_step, 1)
                tt(lnv[:, 2, rows], stats[:, rows, 2], stats[:, rows, 5], ALU.add).then_inc(ln_step, 1)
                dve.wait_ge(ln_step, base + 3)
                nc.vector.tensor_scalar(lnv[:, 0, rows], lnv[:, 0, rows], 0.5, None, ALU.mult).then_inc(ln_step, 1)
                tt(lnv[:, 1, rows], lnv[:, 1, rows], lnv[:, 1, rows], ALU.mult).then_inc(ln_step, 1)
                nc.vector.tensor_scalar(lnv[:, 2, rows], lnv[:, 2, rows], 1.0 / D, EPS, ALU.mult, ALU.add).then_inc(ln_step, 1)
                dve.wait_ge(ln_step, base + 6)
                nc.vector.scalar_tensor_tensor(lnv[:, 3, rows], lnv[:, 1, rows], 0.25, lnv[:, 2, rows], ALU.mult, ALU.add).then_inc(ln_step, 1)

            def inverse_deviations(g, j):
                dve.wait_ge(std_ready, g + 1)
                rows = bass.ds(TQ * j, TQ)
                nc.vector.reciprocal(lnv[:, 5, rows], lnv[:, 4, rows]).then_inc(ln_step, 1)
                dve.wait_ge(ln_step, LN_STEPS * (g + 1))

            def normalized_rows(j, par):
                for t in range(CT):
                    tile = TQ * j + CT * par + t
                    mean, rstd = lnv[:, 0, bass.ds(tile, 1)], lnv[:, 5, bass.ds(tile, 1)]
                    nc.vector.tensor_scalar(xn[:, par, t:t + 1, 0:D], x_sb[:, bass.ds(tile, 1), :], mean, rstd,
                                            ALU.subtract, ALU.mult).then_inc(xn_ready, 1)
                    nc.vector.tensor_scalar(xn[:, par, t, D:XC].rearrange("p (e c) -> p e c", e=2),
                                            x_sb[:, bass.ds(tile, 1), FULL * P:D].to_broadcast([P, 2, REM]), mean, rstd,
                                            ALU.subtract, ALU.mult).then_inc(xn_ready, 1)

            def transposed(cc, ci, par, kind):
                for k in range(3):
                    rows = slice(0, P) if k < FULL else slice(0, RR)
                    dve.wait_ge(t_ready, 3 * cc + k + 1)
                    dve.wait_ge(xl_ready, 3 * (ci - 2) + k + 1 + XL_CREDIT)
                    nc.vector.tensor_scalar(y[rows, par, k, :], ps[rows, k, :], mod_now[rows, k, kind + 1:kind + 2],
                                            mod_now[rows, k, kind:kind + 1], ALU.mult, ALU.add).then_inc(y_ready, 1)

            def modulation_of(j, kind, value):
                for rows, ks in ((slice(0, P), slice(0, FULL)), (slice(0, RR), slice(FULL, 3))):
                    nc.vector.tensor_copy(mod_now[rows, ks, kind:kind + 2],
                                          modv[rows, bass.ds(j, 1), ks, kind:kind + 2].rearrange("p a k g -> p (a k) g")).then_inc(mod_copied, 1)
                dve.wait_ge(mod_copied, value)

            def bias_rows(hi_done, dst_r, src):
                dve.wait_ge(hi_done, 2)
                nc.vector.scalar_tensor_tensor(dst_r[RR:RB, :], dst_r[RR:RB, :].bitcast(f32), ident[RR:RB, RR + 1:RR + 2],
                                               src[RR:RB, ...], ALU.mult, ALU.subtract).then_inc(bias_split, 1)

            def modulations(first, ready, signal):
                dve.wait_ge(ready, 1)
                for b in range(B):
                    for rows, ks in ((slice(0, P), slice(0, FULL)), (slice(0, RR), slice(FULL, 3))):
                        nc.vector.tensor_copy(modv[rows, b, ks, first], mod_ps[rows, ks, first, b]).then_inc(signal, 1)
                        nc.vector.tensor_scalar(modv[rows, b, ks, first + 1], mod_ps[rows, ks, first + 1, b], 1.0, None,
                                                ALU.add).then_inc(signal, 1)

            tile_statistics(0, 0, lambda t: dve.wait_ge(x_in[t // CT], 16))
            variances(0, 0)
            dve.wait_ge(silu_c, 1)
            dve.wait_ge(cond_rows, 2)
            for k in range(NK):
                rows = KC + 1 if k == 0 else KC
                nc.vector.tensor_copy(sc_b[0:rows, k, :, :], sc_t[0:rows, k, :].unsqueeze(2).to_broadcast([rows, B, P])).then_inc(silu_c, 1)
            inverse_deviations(0, 0)
            for par in range(2):
                normalized_rows(0, par)
            modulations(0, mod_mm, mod_ready)
            dve.wait_ge(mod_ready, 4 * B)
            modulation_of(0, 0, 2)
            transposed(0, 0, 0, 0)
            bias_rows(wp_hi, wp_r, wp_stage[:, FULL, :])

            def dve_first(j, last):
                for par in range(2):
                    c = 2 * j + par
                    if par == 0 and not last:
                        for tokens_in in x_in[TQ // CT:]:
                            dve.wait_ge(tokens_in, 16)
                        tile_statistics(j + 1, j + 1, lambda t: None)
                        variances(j + 1, j + 1)
                    for m, rows in enumerate(QKP):
                        dve.wait_ge(qk_hi, 5 * c + m + 1)
                        nc.vector.tensor_tensor(qk_st[0:rows, m, 1, :], ps[0:rows, 3 + m, :], qk_st[0:rows, m, 0, :].bitcast(f32),
                                                ALU.subtract).then_inc(qk_evac, 1)
                    if par == 1 and not last:
                        modulation_of(j + 1, 0, 2 * (j + 2))
                    if par == 0 or not last:
                        transposed(c + 1, c + 1, 1 - par, 0)
                    if par == 0 and not last:
                        inverse_deviations(j + 1, j + 1)
                    for t in range(CT):
                        dve.wait_ge(v_hi, CT * c + t + 1)
                        dve.wait_ge(v_split, CT * c + t - 2 + 1 + VS_CREDIT + 1)
                        nc.vector.tensor_tensor(v_res[:, t % 2, :].rearrange("p (h d) -> p h d", h=H),
                                                ps[:, 3 + t, 0:D].rearrange("p (h d) -> p h d", h=H), v_part(j, par, t)(0),
                                                ALU.subtract).then_inc(v_evac, 1)
                    if not last:
                        normalized_rows(j + 1, par)

            with dve.Fori(0, B - 1) as j:
                dve_first(j, False)
            dve_first(B - 1, True)

            dve.wait_ge(v_ready, TILES)
            dve.wait_ge(wp_split, FULL + 1)
            dve.wait_ge(bias_split, 1)
            nc.vector.memset(k_st[:].bitcast(f32), 1.0).then_inc(ones_ready, 1)
            nc.vector.memset(mneg[:], 0.0).then_inc(ones_ready, 1)
            dve.wait_ge(ones_ready, 2)

            def split_maximum(n, r):
                dve.wait_ge(mt_ready, n + 1)
                nc.vector.tensor_copy(m_t[0:TQ, r, 0, :], slot1[0:TQ, 0:P]).then_inc(mt_hi, 1)
                dve.wait_ge(mt_hi, n + 1)
                nc.vector.tensor_tensor(m_t[0:TQ, r, 1, :], slot1[0:TQ, 0:P], m_t[0:TQ, r, 0, :].bitcast(f32),
                                        ALU.subtract).then_inc(mt_used, 1)

            def vector_lo(n, r, g):
                dve.wait_ge(exp_done, NG * n + g + 1)
                lo_part(nc.vector, n, r, g).then_inc(lo_vector, 1)

            def sums(n, r):
                dve.wait_ge(pv_ready, n + 1)
                dve.wait_ge(ctx_ready, count(n - 2))
                nc.vector.tensor_reduce(csum[:, r, :, :], pv.rearrange("p i (e d) -> p i d e", e=3), axis=AX.X,
                                        op=ALU.add).then_inc(pv_used, 1)
                dve.wait_ge(pv_used, n + 1)
                nc.vector.reciprocal(rden[:, r, :], csum[:, r, :, HD]).then_inc(rden_ready, 1)

            def dve_head(n, r):
                fixed = isinstance(n, int)
                for s, i in enumerate(ORDER):
                    if s == 0 and (not fixed or 1 <= n <= HEADS):
                        split_maximum(n - 1, (r - 1) % 3)
                    if not fixed or n < HEADS:
                        dve.wait_ge(max_ready, TQ * n + s + 1)
                        src = (slot2 if s % 2 == 0 else slot1)[:, 0:(i + 1) * P]
                        nc.vector.tensor_reduce(mneg[:, r, i:i + 1], src, axis=AX.X, op=ALU.max, negate=True).then_inc(max_used, 1)
                    if s in LO_VECTOR_AT and (not fixed or 2 <= n <= HEADS + 1):
                        vector_lo(n - 2, (r - 2) % 3, LO_VECTOR_AT[s])
                    if s == SUMS_AT and (not fixed or 3 <= n <= HEADS + 2):
                        sums(n - 3, r)

            for n in range(FIRST):
                dve_head(n, n % 3)
                if n == 0:
                    dve.wait_ge(gate_mm, 1)
                    for b in range(B):
                        for i in range(2):
                            nc.vector.tensor_copy(gate[:, b, i, :], ps[:, 3 + 2 * b + i, 0:D]).then_inc(gate_ready, 1)
                    modulations(2, mod2_mm, gate_ready)
            with dve.Fori(0, (HEADS - FIRST) // LOOPED) as j:
                for i in range(LOOPED):
                    dve_head(LOOPED * j + FIRST + i, (FIRST + i) % 3)
            def context_lo(cc, par):
                for k in range(3):
                    dve.wait_ge(xh_ready, 3 * cc + k + 1)
                    if k < FULL:
                        nc.vector.tensor_tensor(xl[:, par, k, :], ps[:, k, :], xh[:, par, k, :].bitcast(f32),
                                                ALU.subtract).then_inc(y_ready, 1)
                    else:
                        rows = slice(2 * REM, RR)
                        nc.vector.tensor_tensor(xr[rows, par, :], ps[rows, k, :], xr[rows, par, :].bitcast(f32),
                                                ALU.subtract).then_inc(y_ready, 1)

            for n in range(HEADS, HEADS + 2):
                dve_head(n, n % 3)

            for par in range(2):
                context_lo(2 * B + par, par)
            dve_head(HEADS + 2, (HEADS + 2) % 3)
            dve.wait_ge(w1_hi, 2)
            nc.vector.tensor_tensor(w1_r[REM:2 * REM, :], raw1[REM:2 * REM, FULL, :], w1_r[REM:2 * REM, :].bitcast(f32),
                                    ALU.subtract).then_inc(w1_split, 1)
            bias_rows(w1_hi, w1_r, raw1[:, FULL, :])

            def gated_context(j):
                for t in range(TQ):
                    n = TQ * j + t
                    dve.wait_ge(wp_ready, n + 1)
                    dve.wait_ge(x2_ready, n - 2 + 1 + RES_CREDIT)
                    nc.vector.tensor_tensor(res[:, t % 2:t % 2 + 1, :], ps[:, 3 + t % CT:4 + t % CT, 0:D],
                                            gate[:, bass.ds(j, 1), 0, :], ALU.mult).then_inc(res1_ready, 1)

            with dve.Fori(0, B - 1) as j:
                gated_context(j)
                for par in range(2):
                    context_lo(2 * B + 2 * (j + 1) + par, par)
            tile_statistics(B, 0, lambda t: dve.wait_ge(x2_ready, t + 1 + RES_CREDIT))
            gated_context(B - 1)
            variances(B, 0)
            dve.wait_ge(w2_hi, 2)
            bias_rows(w2_hi, w2_r, raw2b)

            inverse_deviations(B, 0)
            modulation_of(0, 2, 2 * B + 2)
            for par in range(2):
                normalized_rows(0, par)
            transposed(4 * B, 2 * B, 0, 2)

            def dve_mlp(j, last):
                for par in range(2):
                    c = 2 * j + par
                    if par == 0 and not last:
                        tile_statistics(B + j + 1, j + 1, lambda t: dve.wait_ge(x2_ready, TQ * (j + 1) + t + 1 + RES_CREDIT))
                        variances(B + j + 1, j + 1)
                    dve.wait_ge(w2_ready, CT * c)
                    for m in range(MF):
                        dve.wait_ge(h_ready, MF * c + m + 1 + H_CREDIT)
                        nc.vector.tensor_copy(h_h[:, m, :], hs[:, m % 3, :]).then_inc(hh_ready, 1)
                    if par == 1 and not last:
                        modulation_of(j + 1, 2, 2 * B + 2 * (j + 2))
                    if par == 0 or not last:
                        transposed(4 * B + c + 1, 2 * B + c + 1, 1 - par, 2)
                    for t in range(CT):
                        n = CT * c + t
                        dve.wait_ge(w2_ready, n + 1)
                        dve.wait_ge(x3_ready, n - 2 + 1 + RES_CREDIT)
                        nc.vector.tensor_tensor(res[:, t % 2:t % 2 + 1, :], ps[:, 6 + t % 2:7 + t % 2, 0:D],
                                                gate[:, bass.ds(j, 1), 1, :], ALU.mult).then_inc(res2_ready, 1)
                    if not last:
                        if par == 0:
                            inverse_deviations(B + j + 1, j + 1)
                        normalized_rows(j + 1, par)

            with dve.Fori(0, B - 1) as j:
                dve_mlp(j, False)
            dve_mlp(B - 1, True)

        @block.tensor
        def _(pe):
            mm = nc.tensor.matmul

            def modulation_products(first, bank):
                for k in range(3):
                    for g in (first, first + 1):
                        group = (0, 1, 3, 4)[g]
                        at = (k * 4 + g) * B
                        for p0, cols in ([(0, P)] if k < FULL else [(i * REM, REM) for i in range(3)]):
                            for kk in range(NK):
                                rows = KC + 1 if kk == 0 else KC
                                last = mm(ps[p0:p0 + cols, bank, at:at + B],
                                          wa_sb[0:rows, kk, group * D + k * P:group * D + k * P + cols],
                                          sc_t[0:rows, kk, :], start=kk == 0, stop=kk == NK - 1)
                return last

            def gate_products(b, i):
                for kk in range(NK):
                    rows = KC + 1 if kk == 0 else KC
                    group = (2, 5)[i]
                    last = mm(ps[:, 3 + 2 * b + i, 0:D], sc_b[0:rows, kk, b, :], wa_sb[0:rows, kk, group * D:(group + 1) * D],
                              start=kk == 0, stop=kk == NK - 1)
                return last

            pe.wait_ge(wa_in, 32)
            pe.wait_ge(silu_c, 1)
            pe.wait_ge(cond_rows, 2)
            modulation_products(0, MOD_BANK).then_inc(mod_mm, 1)

            def transposes(cc, par):
                pe.wait_ge(xn_ready, 2 * CT * (cc + 1))
                for k in range(3):
                    cols = slice(k * P, (k + 1) * P) if k < FULL else slice(FULL * P, XC)
                    rows = P if k < FULL else RR
                    pe.wait_ge(y_ready, 3 * (cc - 1) + k + 1 + Y_CREDIT)
                    for t in range(CT):
                        last = nc.tensor.transpose(ps[0:rows, k, t * P:(t + 1) * P], xn[:, par, t, cols], ident[:])
                    last.then_inc(t_ready, 1)

            def products(out_ap, terms):
                for i, (lhs, rhs) in enumerate(terms):
                    last = mm(out_ap, lhs, rhs, start=i == 0, stop=i == len(terms) - 1)
                return last

            def weights_first(out_ap, wh, wl, wr, cols, par, rows):
                return products(out_ap, [(w, a) for k in range(FULL) for w, a in (
                    (wh[:, k, cols], xh[:, par, k, :]), (wl[:, k, cols], xh[:, par, k, :]), (wh[:, k, cols], xl[:, par, k, :]))]
                    + [(wr[0:rows, cols], xr[0:rows, par, :])])

            def tokens_first(out_ap, wh, wl, wr, cols, par, t, rows):
                tok = slice(t * P, (t + 1) * P)
                return products(out_ap, [(a, w) for k in range(FULL) for a, w in (
                    (xh[:, par, k, tok], wh[:, k, cols]), (xh[:, par, k, tok], wl[:, k, cols]), (xl[:, par, k, tok], wh[:, k, cols]))]
                    + [(xr[0:rows, par, tok], wr[0:rows, cols])])

            pe.wait_ge(consts_made, 1)
            transposes(0, 0)
            pe.wait_ge(mod_ready, 4 * B)
            pe.wait_ge(wqkv_split, FULL + 1)

            def pe_first(j, last):
                for par in range(2):
                    c = 2 * j + par
                    pe.wait_ge(xl_ready, 3 * (c + 1) + XL_CREDIT)
                    for m, rows in enumerate(QKP):
                        if m < CT:
                            pe.wait_ge(v_evac, CT * (c - 1) + m + 1 + V_CREDIT)
                        else:
                            pe.wait_ge(qk_evac, 5 * c)
                        weights_first(ps[:, 3 + m, :], wqkv_h, wqkv_l, wqkv_r, slice(m * P, (m + 1) * P), par, RR).then_inc(qk_ready, 1)
                    if par == 0 or not last:
                        transposes(c + 1, 1 - par)
                    for t in range(CT):
                        pe.wait_ge(qk_evac, 5 * c + t + 1)
                        tokens_first(ps[:, 3 + t, 0:D], wqkv_h, wqkv_l, wqkv_r, slice(2 * D, 3 * D), par, t, RR).then_inc(v_ready, 1)
                    pe.wait_ge(v_ready, CT * (c + 1))
                    pe.sem_inc(xt_used, 1)

            with pe.Fori(0, B - 1) as j:
                pe_first(j, False)
            pe_first(B - 1, True)

            pe.wait_ge(y_ready, 3 * 2 * B + Y_CREDIT)
            pe.wait_ge(qk_evac, 5 * 2 * B)
            pe.wait_ge(v_evac, TILES + V_CREDIT)
            pe.wait_ge(wa_rest_in, 16)
            pe.wait_ge(silu_c, 1 + NK)

            def pe_head(n, r, k3, place_of):
                fixed = isinstance(n, int)
                q, k = stack(q_st, r), stack(k_st, r)
                if fixed and n == WARM_AT:
                    warm = v_sb[:, 0, :, :].rearrange("p k c -> p (k c)")
                    for _ in range(8):
                        mm(ps[:, 7, 0:TQ * 3 * VP], ident_b[:], warm, start=True, stop=True)
                scores, maxima = not fixed or n < HEADS, not fixed or 1 <= n <= HEADS
                values = not fixed or 3 <= n <= HEADS + 2
                for s, i in enumerate(ORDER):
                    if scores:
                        if s == 0:
                            pe.wait_ge(stacks_in[r], 6 * 16 * (k3 + 1))
                        pe.wait_ge(max_used, count(TQ * n + s - 1))
                        if s == 1:
                            pe.wait_ge(mt_used, n)
                        slot = slot2 if s % 2 == 0 else slot1
                        for c0 in range(0, (i + 1) * P, CHUNK):
                            c1 = min(c0 + CHUNK, (i + 1) * P)
                            mm(slot[:, c0:c1], q[0:SR, i * P:(i + 1) * P], k[0:SR, c0:c1], start=True, stop=c1 < (i + 1) * P)
                        mm(slot[:, i * P:(i + 1) * P], ident_b[:], mask[:], start=False, stop=True).then_inc(max_ready, 1)
                    if s == 0 and maxima:
                        pe.wait_ge(max_used, TQ * n)
                        nc.tensor.transpose(slot1[:, 0:P], mneg[:, (r - 1) % 3, :], ident[:]).then_inc(mt_ready, 1)
                    if fixed and n == 0 and s < 2 * B:
                        last = gate_products(s // 2, s % 2)
                        if s == 2 * B - 1:
                            last.then_inc(gate_mm, 1)
                    if fixed and n == 0 and s == TQ - 1:
                        modulation_products(2, MOD_BANK).then_inc(mod2_mm, 1)
                    if fixed and n == 1 and s == 0:
                        pe.wait_ge(gate_ready, 2 * B + 4 * B)
                        pe.wait_ge(v_split, TILES + 1 + VS_CREDIT)
                    if values:
                        for tile in VALUES_AT[s]:
                            weighted_values(n - 3, r, tile)
                    if maxima and s in SCORES_T_AT:
                        transposed_scores(n - 1, (r - 1) % 3, k3 if r else k3 - 1, SCORES_T_AT[s], place_of - 1)

            def transposed_scores(n, r, k3, g, place_of):
                q, k = stack(q_st, r), stack(k_st, r)
                slot = slot_of(place_of, g)
                if g == 0:
                    pe.wait_ge(m_rows[r], 2 * 16 * (k3 + 1))
                pe.wait_ge(exp_done, count(NG * n + g - 1))
                for kt in GROUPS[g]:
                    at = KOFF[kt] - GOFF[g]
                    c0 = 0
                    while c0 < L - P * kt:
                        c1 = min((at + c0) // CHUNK * CHUNK + CHUNK - at, L - P * kt)
                        mm(slot[:, at + c0:at + c1], k[:, kt * P:(kt + 1) * P], q[:, kt * P + c0:kt * P + c1],
                           start=(at + c0) % CHUNK == 0, stop=c0 > 0, skip_group_check=True)
                        c0 = c1
                    last = mm(slot[:, at:at + P], ident_b[:], mask_t[:], start=False, stop=True, skip_group_check=True)
                last.then_inc(st_ready, 1)

            def weighted_values(n, r, i):
                if i == 0:
                    pe.wait_ge(pv_used, n)
                for signal, groups in ((lo_vector, VECTOR_LOS), (lo_pool, POOL_LOS)):
                    done = max([groups.index(GROUP_OF[kt]) + 1 for kt in range(i + 1) if GROUP_OF[kt] in groups], default=0)
                    if done:
                        pe.wait_ge(signal, len(groups) * n + done)
                for kt in range(i + 1):
                    cols = slice(KOFF[kt] + (i - kt) * P, KOFF[kt] + (i - kt + 1) * P)
                    v = v_sb[:, bass.ds(n, 1), kt, :]
                    hi = pt[r][:, cols].bitcast(bf16).rearrange("p (n e) -> p n e", e=2)[:, :, 1]
                    mm(pv[:, i:i + 1, :], hi, v, start=kt == 0, stop=False)
                    last = mm(pv[:, i:i + 1, :], pt_lo[r][:, cols], v, start=False, stop=kt == i)
                if i == TQ - 1:
                    last.then_inc(pv_ready, 1)

            for n in range(FIRST):
                pe_head(n, n % 3, n // 3, n)
            with pe.Fori(0, (HEADS - FIRST) // LOOPED) as j:
                for i in range(LOOPED):
                    pe_head(LOOPED * j + FIRST + i, (FIRST + i) % 3, LOOPED // 3 * j + (FIRST + i) // 3, FIRST + i)
            for n in range(HEADS, HEADS + 2):
                pe_head(n, n % 3, n // 3, n)

            pe.wait_ge(mt_used, HEADS)
            for par in range(2):
                transposes(2 * B + par, par)
            pe_head(HEADS + 2, (HEADS + 2) % 3, (HEADS + 2) // 3, HEADS + 2)
            pe.wait_ge(exp_done, NG * HEADS)

            def projection(j):
                for par in range(2):
                    c = 2 * j + par
                    pe.wait_ge(y_ready, 3 * (2 * B + c + 1) + Y_CREDIT)
                    for t in range(CT):
                        pe.wait_ge(res1_ready, CT * (c - 1) + t + 1 + WP_CREDIT)
                        tokens_first(ps[:, 3 + t, 0:D], wp_h, wp_l, wp_r, slice(0, D), par, t, RB).then_inc(wp_ready, 1)
                    pe.wait_ge(wp_ready, CT * (c + 1))
                    pe.sem_inc(xt_used, 1)

            with pe.Fori(0, B - 1) as j:
                projection(j)
                for par in range(2):
                    transposes(2 * B + 2 * (j + 1) + par, par)
            projection(B - 1)

            transposes(4 * B, 0)
            pe.wait_ge(res1_ready, TILES + WP_CREDIT)
            pe.wait_ge(pv_used, HEADS)
            pe.wait_ge(w1_split, FULL + 1)
            pe.wait_ge(bias_split, 3)

            def pe_mlp(j, last):
                for par in range(2):
                    c = 2 * j + par
                    pe.wait_ge(xl_ready, 3 * (2 * B + c + 1) + XL_CREDIT)
                    for m in range(MF):
                        pe.wait_ge(h_ready, MF * c + m - 3 + 1 + H_CREDIT)
                        weights_first(ps[:, 3 + m % 3, :], w1_h, w1_l, w1_r, slice(m * P, (m + 1) * P), par, RB).then_inc(w1_ready, 1)
                    pe.wait_ge(w1_ready, MF * (c + 1))
                    pe.sem_inc(xt_used, 1)
                    if par == 0 or not last:
                        transposes(4 * B + c + 1, 1 - par)
                    for t in range(CT):
                        n = CT * c + t
                        tok = slice(t * P, (t + 1) * P)
                        pe.wait_ge(res2_ready, n - 2 + 1 + W2_CREDIT)
                        pe.wait_ge(w2_split, 1)
                        for m in range(MF):
                            if t == 0:
                                pe.wait_ge(hl_ready, MF * c + m + 1 + HS_CREDIT)
                            for i, (a, w) in enumerate(((h_h, w2_h), (h_h, w2_l), (h_l, w2_h))):
                                mm(ps[:, 6 + t % 2, 0:D], a[:, m, tok], w[:, m, :], start=m == 0 and i == 0, stop=False)
                        mm(ps[:, 6 + t % 2, 0:D], minus1[RR:RB, :], w2_r[RR:RB, :], start=False, stop=True).then_inc(w2_ready, 1)

            with pe.Fori(0, B - 1) as j:
                pe_mlp(j, False)
            pe_mlp(B - 1, True)


_INPUTS = ["x", "cond_1152", "L0_cond_Wq", "L0_cond_Wk", "L0_cond_Wv", "L0_cond_Wp", "L0_cond_bp", "L0_cond_W1",
           "L0_cond_b1", "L0_cond_W2", "L0_cond_b2", "L0_cond_Wa", "L0_cond_ba"]


def kernel(**inputs):
    import concourse.bacc as bacc
    from concourse.bass_utils import run_bass_kernel_spmd

    nc = bacc.Bacc("TRN2", target_bir_lowering=False, num_devices=1)
    arrays, args = {}, []
    for name in _INPUTS:
        a = np.ascontiguousarray(inputs[name])
        arrays[f"in_{name}"] = a
        args.append(nc.dram_tensor(f"in_{name}", a.shape, mybir.dt.from_np(a.dtype), kind="ExternalInput").ap())
    out = nc.dram_tensor("out", arrays["in_x"].shape, mybir.dt.float32, kind="ExternalOutput").ap()
    conditioned_transformer_block(nc, *args, out)
    r = run_bass_kernel_spmd(nc, [arrays], core_ids=[0])
    return r.results[0]["out"]
```

```python
import numpy as np
import concourse.bass as bass
from concourse import mybir


def conditioned_transformer_block(nc, x, cond, Wq, Wk, Wv, Wp, bp, W1, b1, W2, b2, Wa, ba, out):
    f32, f32r, bf16, f16 = mybir.dt.float32, mybir.dt.float32r, mybir.dt.bfloat16, mybir.dt.float16
    ALU, ACT, AX = mybir.AluOpType, mybir.ActivationFunctionType, mybir.AxisListType

    B, L, D = x.shape
    P = nc.NUM_PARTITIONS
    H = 16
    HD = D // H
    F = W1.shape[1]
    EPS = 1e-6
    SCALE = 1.0 / float(np.sqrt(HD))
    NEG = -1e30
    TILES = B * L // P
    TQ = L // P
    CHUNK = 512
    CT = CHUNK // P
    FULL = D // P
    REM = D - FULL * P
    XC = D + 2 * REM
    RR = 3 * REM
    RB = RR + 2
    MF = F // P
    QKP = [P, P, P, P, 2 * D - 4 * P]
    QK_RUNS = [[(max(a, lo) - a, min(a + rows, hi) - max(a, lo), w, max(a, lo) - lo)
                for w, (lo, hi) in enumerate(((0, D), (D, 2 * D))) if max(a, lo) < min(a + rows, hi)]
               for a, rows in zip(range(0, 5 * P, P), QKP)]
    HEADS = B * H
    SR = 3 * HD
    SM = SR + 2
    VP = HD + 1
    KC = 96
    NK = D // KC

    GROUPS = [[0], [1, 7], [2, 6], [3, 5], [4]]
    GW = [sum(L - P * kt for kt in g) for g in GROUPS]
    GOFF = [sum(GW[:g]) for g in range(len(GROUPS))]
    NG = len(GROUPS)
    PCOLS = sum(GW)
    KOFF = {}
    for g, kts in enumerate(GROUPS):
        at = GOFF[g]
        for kt in kts:
            KOFF[kt] = at
            at += L - P * kt
    ORDER = [7, 3, 6, 2, 5, 1, 4, 0]
    VALUES_AT = [[2, 3, 4], [5], [6, 7], [], [], [], [], []]
    EARLY_VALUES = [0, 1]
    SCORES_T_AT = [[], [], [0], [1], [2], [3], [4], []]
    LO_VECTOR_AT, SUMS_AT = {1: 1}, 3
    WARM_AT = 3
    STATS_LAG = 3
    NEXT_AT = 2
    LN_STEPS = TQ + 8
    LOOPED = 6
    FIRST = HEADS % LOOPED + LOOPED
    GROUP_OF = {kt: g for g, kts in enumerate(GROUPS) for kt in kts}
    VECTOR_LOS, POOL_LOS = [1], [0, 2, 3, 4]
    LAST_LOS = [1, 3, 4], [0, 2]

    qk_dram = nc.dram_tensor("qk_scratch", [2, 2, B * D, L], f32).ap()

    cursor = [nc.sbuf_base + 63 & ~63]

    def place(name, shape, dt, at=None):
        size = int(np.prod(shape[1:])) * (2 if dt in (bf16, f16) else 4)
        where = cursor[0] if at is None else at[0]
        t = nc.alloc_sbuf_tensor_at(name, shape, dt, offset=where)
        (cursor if at is None else at)[0] = where + (size + 31 & ~31)
        return t

    x_sb = place("x_sb", [P, TILES, D], f32)
    ctx_at = [cursor[0]]
    ctx_sb = place("ctx_sb", [P, TQ, B, D], f32)
    gate = place("gate", [P, B, 2, D], f32)
    modv = place("modv", [P, B, 3, 4], f32)
    mod_now = place("mod_now", [P, 3, 4], f32)
    stats = place("stats", [P, TILES, 6], f32)
    lnv = place("lnv", [P, 6, TILES], f32)
    pt3_at = [cursor[0]]
    xn = place("xn", [P, 2, CT, XC], f32)
    y = place("y", [P, 2, 3, CHUNK], f32)
    xh = place("xh", [P, 2, FULL, CHUNK], f32r)
    xl = place("xl", [P, 2, FULL, CHUNK], f32r)
    xr = place("xr", [P, 2, CHUNK], f32r)
    minus1 = place("minus1", [P, P], f32r)
    ident = place("ident", [P, P], f32)
    ident_b = place("ident_b", [P, P], bf16)
    mask = place("mask", [P, P], bf16)
    mask_t = place("mask_t", [P, P], bf16)
    wp_h = place("wp_h", [P, FULL, D], f32r)
    wp_l = place("wp_l", [P, FULL, D], f32r)
    wp_r = place("wp_r", [P, D], f32r)
    res = place("res", [P, CT, D], f32)
    area = cursor[0]

    a1 = [area]
    wqkv_h = place("wqkv_h", [P, FULL, 3 * D], f32r, a1)
    wqkv_l = place("wqkv_l", [P, FULL, 3 * D], f32r, a1)
    wqkv_r = place("wqkv_r", [P, 3 * D], f32r, a1)
    raw = place("raw", [P, 3, 4 * D], f32, a1)
    qk_st = place("qk_st", [P, 5, 2, CHUNK], f32r, a1)
    wa_sb = place("wa_sb", [P, NK, 6 * D], f32, a1)
    c_t = place("c_t", [P, NK, B], f32, a1)
    sc_t = place("sc_t", [P, NK, B], f32, a1)
    sc_b = place("sc_b", [P, NK, B, P], f32, a1)

    a2 = [area]
    q_st = place("q_st", [P, 2, L], f32r, a2)
    k_st = place("k_st", [P, 2, L], f32r, a2)
    mneg = place("mneg", [P, 3, P], f32, a2)
    m_t = place("m_t", [P, 3, 2, P], f32r, a2)
    csum = place("csum", [P, 3, TQ, VP], f32, a2)
    rden = place("rden", [P, 3, TQ], f32, a2)
    stacks_end = a2[0]
    pt = [place(f"pt{i}", [P, PCOLS], f32, a2 if i < 2 else pt3_at) for i in range(3)]
    pt_lo = [place(f"pt_lo{i}", [P, PCOLS], f16, a2 if i < 2 else pt3_at) for i in range(3)]

    a3 = [area]
    w1_h = place("w1_h", [P, FULL, F], f32r, a3)
    w1_r = place("w1_r", [P, F], f32r, a3)
    w2_r = place("w2_r", [P, D], f32r, a3)
    assert a3[0] <= area + 2 * 2 * L * 4
    a3 = [stacks_end]
    w1_l = place("w1_l", [P, FULL, F], f32r, a3)
    h_h = place("h_h", [P, MF, CHUNK], f32r, a3)
    h_l = place("h_l", [P, MF, CHUNK], f32r, ctx_at)
    w2_h = place("w2_h", [P, MF, D], f32r, a3)
    w2_l = place("w2_l", [P, MF, D], f32r, a3)

    v_at = max(a1[0], a2[0], a3[0])
    av = [v_at]
    v_sb = place("v_sb", [P, HEADS, TQ, 3 * VP], bf16, av)
    v_res = place("v_res", [P, 2, D], f32, av)
    ones = place("ones", [P, P], f32r, av)
    ar = [v_at]
    raw1 = place("raw1", [P, 3, F], f32, ar)
    raw2 = place("raw2", [P, MF, D], f32, ar)
    raw2b = place("raw2b", [P, D], f32, ar)
    hs = place("hs", [P, 3, CHUNK], f32, ar)
    V_HEADS_1 = -(-3 * F * 4 // (TQ * 3 * VP * 2))
    V_HEADS_2 = -(-(3 * F + MF * D + D) * 4 // (TQ * 3 * VP * 2))
    assert V_HEADS_2 <= HEADS - 3
    assert max(av[0], ar[0]) <= nc.sbuf_usable_end, (av[0], ar[0], nc.sbuf_usable_end)

    from contextlib import ExitStack
    with ExitStack() as ctx:
        ps = ctx.enter_context(nc.psum_tensor("ps", [P, 8, 512], f32))

        def sem(name):
            return ctx.enter_context(nc.semaphore(name))

        x_in = [sem(f"x_in{c}") for c in range(B * L // CHUNK)]
        wqkv_rest, wp_rest, w1_rest = sem("wqkv_rest"), sem("wp_rest"), sem("w1_rest")
        wa_rest_in, ones_in, mod2_ready = sem("wa_rest_in"), sem("ones_in"), sem("mod2_ready")
        cond_in, wa_in, wqkv_in, wp_in, w1_in, w2_in = (sem(n) for n in (
            "cond_in", "wa_in", "wqkv_in", "wp_in", "w1_in", "w2_in"))
        pool_made, consts_made, silu_c, cond_rows, mod_mm, mod_ready, gate_mm, gate_ready = (sem(n) for n in (
            "pool_made", "consts_made", "silu_c", "cond_rows", "mod_mm", "mod_ready", "gate_mm", "gate_ready"))
        bias_split, mod2_mm = sem("bias_split"), sem("mod2_mm")
        wqkv_hi, wqkv_split, wp_hi, wp_split, w1_hi, w1_split, w2_hi, w2_split = (sem(n) for n in (
            "wqkv_hi", "wqkv_split", "wp_hi", "wp_split", "w1_hi", "w1_split", "w2_hi", "w2_split"))
        ln_step, std_ready, mod_copied, xn_ready, t_ready, y_ready, xh_ready, xl_ready, xt_used = (sem(n) for n in (
            "ln_step", "std_ready", "mod_copied", "xn_ready", "t_ready", "y_ready", "xh_ready", "xl_ready", "xt_used"))
        qk_ready, qk_hi, qk_evac, v_ready, v_hi, v_evac, v_mid, v_split = (sem(n) for n in (
            "qk_ready", "qk_hi", "qk_evac", "v_ready", "v_hi", "v_evac", "v_mid", "v_split"))
        qk_out = [sem(f"qk_out{m}") for m in range(5)]
        stacks_in = [sem(f"stacks_in{r}") for r in range(3)]
        m_rows = [sem(f"m_rows{r}") for r in range(3)]
        ones_ready, max_ready, max_used, mt_ready, mt_hi, mt_used, st_ready, exp_done = (sem(n) for n in (
            "ones_ready", "max_ready", "max_used", "mt_ready", "mt_hi", "mt_used", "st_ready", "exp_done"))
        lo_vector, lo_pool, pv_ready, pv_used, rden_ready, ctx_ready = (sem(n) for n in (
            "lo_vector", "lo_pool", "pv_ready", "pv_used", "rden_ready", "ctx_ready"))
        wp_ready, res1_ready, x2_ready, w1_ready, h_ready, hh_ready, hl_ready, w2_ready, res2_ready, x3_ready = (
            sem(n) for n in ("wp_ready", "res1_ready", "x2_ready", "w1_ready", "h_ready", "hh_ready", "hl_ready",
                             "w2_ready", "res2_ready", "x3_ready"))
        out_done = sem("out_done")

        block = ctx.enter_context(nc.Block())

        def count(v):
            return max(v, 0) if isinstance(v, int) else v

        x_tok = x.rearrange("b l d -> (b l) d")
        out_tok = out.rearrange("b l d -> (b l) d")
        slot2 = ps[:, 0:2, :].rearrange("p a c -> p (a c)")
        slot1 = ps[:, 2, :]
        st_slot = [ps[:, 3:5, :].rearrange("p a c -> p (a c)"), ps[:, 5:7, :].rearrange("p a c -> p (a c)")]
        pv = ps[:, 7, 0:TQ * 3 * VP].rearrange("p (i c) -> p i c", i=TQ)

        Y_CREDIT, XL_CREDIT, XT_CREDIT, V_CREDIT, VS_CREDIT = 3, 6, 2, CT, 2
        WP_CREDIT, RES_CREDIT, H_CREDIT, HS_CREDIT, W2_CREDIT = CT, CT, 3, 3, 2

        MOD_BANK, MOD2_BANK, GATE_BANKS = 7, 3, [0, 1, 2, 7]

        def v_part(j, par, t):
            return lambda i: v_sb[:, bass.ds(H * j, H), CT * par + t, i * VP:i * VP + HD]

        def lo_part(engine, n, r, g):
            cols = slice(GOFF[g], GOFF[g] + GW[g])
            w = pt[r][:, cols]
            return engine.tensor_tensor(pt_lo[r][:, cols], w, w.bitcast(bf16).rearrange("p (n e) -> p n e", e=2)[:, :, 1],
                                        ALU.subtract)

        def slot_of(i, g):
            return st_slot[(NG * i + g) % 2]

        wp_stage = raw[:, :, 3 * D:4 * D]

        def stack(tensor, r):
            return tensor[64 * (r % 2):64 * (r % 2) + SM, r // 2, :]

        def load_weight(eng, dst, src, signal):
            n = src.shape[1]
            eng.dma_start(dst[:, 0:FULL, 0:n], src[0:FULL * P, :].rearrange("(k p) n -> p k n", p=P)).then_inc(signal, 16)
            for i in range(3):
                eng.dma_start(dst[i * REM:(i + 1) * REM, FULL, 0:n], src[FULL * P:D, :]).then_inc(signal, 16)

        def load_bias(eng, dst, src, signal):
            for i in range(2):
                eng.dma_start(dst[i:i + 1, :], src.rearrange("(a n) -> a n", a=1)).then_inc(signal, 16)

        @block.sync
        def _(sp):
            def load_tokens(c):
                sp.dma_start(x_sb[:, c * CT:(c + 1) * CT, :],
                             x_tok[c * CHUNK:(c + 1) * CHUNK, :].rearrange("(t p) d -> p t d", p=P)).then_inc(x_in[c], 16)

            for c in range(TQ // CT):
                load_tokens(c)
            for i, w in enumerate((Wq, Wk, Wv)):
                load_weight(sp, raw[:, :, i * D:(i + 1) * D], w, wqkv_in)
            load_weight(sp, wp_stage, Wp, wp_in)
            load_bias(sp, wp_stage[RR:RB, FULL, :], bp, wp_in)
            for c in range(TQ // CT, TILES // CT):
                load_tokens(c)

            with sp.Fori(0, B) as j:
                for par in range(2):
                    for m, rows in enumerate(QKP):
                        sp.wait_ge(qk_evac, 5 * (2 * j + par) + m + 1)
                        for at, n, which, col in QK_RUNS[m]:
                            sp.dma_start(qk_dram[:, which, bass.ds(D * j + col, n), par * CHUNK:(par + 1) * CHUNK].rearrange("e r c -> r e c"),
                                         qk_st[at:at + n, m, :, :].bitcast(f32)).then_inc(qk_out[m], 16)

            def load_stacks(n, r):
                q, k = stack(q_st, r).bitcast(f32), stack(k_st, r).bitcast(f32)
                for part, (qe, ke) in enumerate(((0, 0), (1, 0), (0, 1))):
                    to = slice(part * HD, (part + 1) * HD)
                    sp.dma_start(q[to, :], qk_dram[qe, 0, bass.ds(n * HD, HD), :]).then_inc(stacks_in[r], 16)
                    sp.dma_start(k[to, :], qk_dram[ke, 1, bass.ds(n * HD, HD), :]).then_inc(stacks_in[r], 16)

            def maximum_rows(n, r):
                for e, in_place in enumerate((mt_hi, mt_used)):
                    sp.wait_ge(in_place, n + 1)
                    sp.dma_start(stack(q_st, r)[SR + e:SR + e + 1, :].bitcast(f32),
                                 m_t[0:TQ, r, e, :].bitcast(f32)).then_inc(m_rows[r], 16)

            for m in range(5):
                sp.wait_ge(qk_out[m], 16 * len(QK_RUNS[m]) * (B * L // CHUNK))
            sp.wait_ge(v_ready, TILES)
            load_stacks(0, 0)
            sp.wait_ge(ones_ready, 1)
            for r in range(3):
                sp.dma_start(stack(k_st, r)[SR:SM, :].bitcast(f32).rearrange("e (i c) -> e i c", i=TQ),
                             ones[0:2, :].bitcast(f32).unsqueeze(1).to_broadcast([2, TQ, P])).then_inc(ones_in, 16)
            load_stacks(1, 1)

            def sp_head(n, r):
                if not isinstance(n, int) or 1 <= n <= HEADS:
                    maximum_rows(n - 1, (r - 1) % 3)
                if not isinstance(n, int) or 2 <= n and n + 1 < HEADS:
                    sp.wait_ge(st_ready, count(NG * (n - 1)))
                    load_stacks(n + 1, (r + 1) % 3)

            load_stacks(2, 2)
            for n in range(FIRST):
                sp_head(n, n % 3)
            with sp.Fori(0, (HEADS - FIRST) // LOOPED - 1) as j:
                for i in range(LOOPED):
                    sp_head(LOOPED * j + FIRST + i, (FIRST + i) % 3)
            sp.wait_ge(pv_ready, V_HEADS_1)
            load_weight(sp, raw1, W1, w1_in)
            load_bias(sp, raw1[RR:RB, FULL, :], b1, w1_in)
            for n in range(HEADS - LOOPED, HEADS + 1):
                sp_head(n, n % 3)
            sp.wait_ge(pv_ready, V_HEADS_2)
            sp.dma_start(raw2[:, :, :], W2.rearrange("(m p) n -> p m n", p=P)).then_inc(w2_in, 16)
            load_bias(sp, raw2b[RR:RB, :], b2, w2_in)

            with sp.Fori(0, B) as j:
                for par in range(2):
                    sp.wait_ge(x3_ready, CT * (2 * j + par + 1) + RES_CREDIT)
                    sp.dma_start(out_tok[bass.ds((2 * j + par) * CHUNK, CHUNK), :].rearrange("(t p) d -> p t d", p=P),
                                 x_sb[:, bass.ds((2 * j + par) * CT, CT), :]).then_inc(out_done, 16)
            sp.wait_ge(out_done, 16 * B * L // CHUNK)

        @block.gpsimd
        def _(pool):
            made = [0]

            def then_made(instruction):
                made[0] += 1
                instruction.then_inc(pool_made, 1)

            then_made(nc.gpsimd.memset(ident[:], 0.0))
            then_made(nc.gpsimd.memset(mask[:], 0.0))
            then_made(nc.gpsimd.memset(mask_t[:], 0.0))
            pool.wait_ge(pool_made, 3)
            then_made(nc.gpsimd.affine_select(out=ident[:], in_=ident[:], compare_op=ALU.not_equal, fill=1.0,
                                              base=0, pattern=[[-1, P]], channel_multiplier=1))
            then_made(nc.gpsimd.affine_select(out=mask[:], in_=mask[:], compare_op=ALU.is_ge, fill=NEG,
                                              base=0, pattern=[[-1, P]], channel_multiplier=1))
            then_made(nc.gpsimd.affine_select(out=mask_t[:], in_=mask_t[:], compare_op=ALU.is_ge, fill=NEG,
                                              base=0, pattern=[[1, P]], channel_multiplier=-1))
            pool.wait_ge(pool_made, 6)
            nc.gpsimd.tensor_copy(ident_b[:], ident[:]).then_inc(consts_made, 1)

            def split_weight(hi_done, split, dst_h, dst_l, src, n):
                for k in range(FULL):
                    pool.wait_ge(hi_done, k + 1)
                    nc.gpsimd.tensor_tensor(dst_l[:, k, :], src[:, k, 0:n], dst_h[:, k, :].bitcast(f32), ALU.subtract).then_inc(split, 1)

            def lo_of_transposed(cc, ci, par):
                for k in range(3):
                    pool.wait_ge(xh_ready, 3 * cc + k + 1)
                    if k < FULL:
                        nc.gpsimd.tensor_tensor(xl[:, par, k, :], y[:, par, k, :], xh[:, par, k, :].bitcast(f32),
                                                ALU.subtract).then_inc(xl_ready, 1)
                    else:
                        rows = slice(2 * REM, RR)
                        pool.wait_ge(xl_ready, 3 * ci + k + XL_CREDIT)
                        nc.gpsimd.tensor_tensor(xr[rows, par, :], y[rows, par, k, :], xr[rows, par, :].bitcast(f32),
                                                ALU.subtract).then_inc(xl_ready, 1)
                pool.wait_ge(xl_ready, 3 * (ci + 1) + XL_CREDIT)

            split_weight(wqkv_hi, wqkv_split, wqkv_h, wqkv_l, raw, 3 * D)
            pool.dma_start(wa_sb[0:KC, :, 2 * D:], Wa[:, 2 * D:].rearrange("(k p) n -> p k n", p=KC)).then_inc(wa_rest_in, 16)
            split_weight(wp_hi, wp_split, wp_h, wp_l, wp_stage, D)

            def pool_first(j, last):
                for par in range(2):
                    if par == 0 or not last:
                        lo_of_transposed(2 * j + par + 1, 2 * j + par + 1, 1 - par)
                    for t in range(CT):
                        dst = v_part(j, par, t)
                        pool.wait_ge(v_mid, CT * (2 * j + par) + t + 1)
                        nc.gpsimd.tensor_tensor(dst(2), v_res[:, t % 2, :].rearrange("p (h d) -> p h d", h=H), dst(1),
                                                ALU.subtract).then_inc(v_split, 1)

            with pool.Fori(0, B - 1) as j:
                pool_first(j, False)
            pool_first(B - 1, True)

            def pool_lo(n, r, g):
                pool.wait_ge(exp_done, NG * n + g + 1)
                lo_part(nc.gpsimd, n, r, g).then_inc(lo_pool, 1)

            def pool_head(n, r):
                if not isinstance(n, int) or 2 <= n <= HEADS:
                    pool_lo(n - 2, (r - 2) % 3, 3)
                if not isinstance(n, int) or 2 <= n <= HEADS:
                    pool_lo(n - 2, (r - 2) % 3, 4)
                if not isinstance(n, int) or 1 <= n <= HEADS + 0:
                    pool_lo(n - 1, (r - 1) % 3, 0)
                if not isinstance(n, int) or 3 <= n <= HEADS + 2:
                    m = n - 3
                    pool.wait_ge(rden_ready, m + 1)
                    nc.gpsimd.tensor_tensor(
                        ctx_sb[:, :, :, :].rearrange("p i b d -> p i (b d)")[:, :, bass.ds(m * HD, HD)],
                        csum[:, r, :, 0:HD], rden[:, r, :].unsqueeze(2).to_broadcast([P, TQ, HD]), ALU.mult).then_inc(ctx_ready, 1)
                if not isinstance(n, int) or 1 <= n <= HEADS + 0:
                    pool_lo(n - 1, (r - 1) % 3, 2)

            for n in range(FIRST):
                pool_head(n, n % 3)
            with pool.Fori(0, (HEADS - FIRST) // LOOPED) as j:
                for i in range(LOOPED):
                    pool_head(LOOPED * j + FIRST + i, (FIRST + i) % 3)
            for n in range(HEADS, HEADS + 2):
                pool_head(n, n % 3)

            pool.wait_ge(pv_ready, HEADS - 1)
            split_weight(w1_hi, w1_split, w1_h, w1_l, raw1, F)
            pool_head(HEADS + 2, (HEADS + 2) % 3)

            def add_context(j):
                for t in range(TQ):
                    pool.wait_ge(res1_ready, TQ * j + t + 1 + WP_CREDIT)
                    xt = x_sb[:, bass.ds(TQ * j + t, 1), :]
                    nc.gpsimd.tensor_tensor(xt, xt, res[:, t % CT:t % CT + 1, :], ALU.add).then_inc(x2_ready, 1)

            with pool.Fori(0, B - 1) as j:
                add_context(j)
            pool.wait_ge(w2_hi, 1)
            nc.gpsimd.tensor_tensor(w2_l[:, :, :], raw2[:, :, :], w2_h[:, :, :].bitcast(f32), ALU.subtract).then_inc(w2_split, 1)
            add_context(B - 1)

            def pool_mlp(j, last):
                for par in range(2):
                    c = 2 * j + par
                    for m in range(MF):
                        pool.wait_ge(hh_ready, MF * c + m + 1)
                        nc.gpsimd.tensor_tensor(h_l[:, m, :], hs[:, m % 3, :], h_h[:, m, :].bitcast(f32),
                                                ALU.subtract).then_inc(hl_ready, 1)
                    if par == 0 or not last:
                        lo_of_transposed(8 + c + 1, 4 + c + 1, 1 - par)
                    for t in range(CT):
                        pool.wait_ge(res2_ready, CT * c + t + 1 + W2_CREDIT)
                        xt = x_sb[:, bass.ds(TQ * j + CT * par + t, 1), :]
                        nc.gpsimd.tensor_tensor(xt, xt, res[:, t:t + 1, :], ALU.add).then_inc(x3_ready, 1)

            with pool.Fori(0, B - 1) as j:
                pool_mlp(j, False)
            pool_mlp(B - 1, True)

        @block.scalar
        def _(act):
            for k in range(NK):
                with nc.allow_non_contiguous_dma(reason="the conditioning vector, a few hundred numbers"):
                    act.dma_start(c_t[0:KC, k, :], cond[:, k * KC:(k + 1) * KC].rearrange("b p -> p b")).then_inc(cond_in, 16)
            act.dma_start(wa_sb[0:KC, :, 0:2 * D], Wa[:, 0:2 * D].rearrange("(k p) n -> p k n", p=KC)).then_inc(wa_in, 16)
            act.dma_start(wa_sb[KC:KC + 1, 0, :], ba.rearrange("(a n) -> a n", a=1)).then_inc(wa_in, 16)
            act.wait_ge(cond_in, 16 * NK)
            act.wait_ge(cond_rows, 1)
            nc.scalar.activation(sc_t[0:KC, :, :], c_t[0:KC, :, :], ACT.Silu).then_inc(silu_c, 1)

            def round_weight(loaded, value, hi_done, dst_h, dst_r, src, n, rows):
                act.wait_ge(loaded, value)
                for k in range(FULL):
                    nc.scalar.activation(dst_h[:, k, :], src[:, k, 0:n], ACT.Copy).then_inc(hi_done, 1)
                nc.scalar.activation(dst_r[0:rows, :], src[0:rows, FULL, 0:n], ACT.Copy).then_inc(hi_done, 1)

            def standard_deviation(g, j):
                act.wait_ge(ln_step, LN_STEPS * g + LN_STEPS - 1)
                rows = bass.ds(TQ * j, TQ)
                nc.scalar.activation(lnv[:, 4, rows], lnv[:, 3, rows], ACT.Sqrt).then_inc(std_ready, 1)

            def hi_of_transposed(cc, par, from_psum=False):
                act.wait_ge(xt_used, cc - 2 + 1 + XT_CREDIT)
                for k in range(3):
                    if from_psum:
                        act.wait_ge(t_ready, 3 * cc + k + 1)
                    else:
                        act.wait_ge(y_ready, 3 * cc + k + 1 + Y_CREDIT)
                    rows = slice(0, P) if k < FULL else slice(0, RR)
                    src = ps[rows, k, :] if from_psum else y[rows, par, k, :]
                    nc.scalar.activation(xh[:, par, k, :] if k < FULL else xr[rows, par, :], src, ACT.Copy).then_inc(xh_ready, 1)

            standard_deviation(0, 0)
            round_weight(wqkv_in, 12 * 16, wqkv_hi, wqkv_h, wqkv_r, raw, 3 * D, RR)
            round_weight(wp_in, 6 * 16, wp_hi, wp_h, wp_r, wp_stage, D, RB)
            hi_of_transposed(0, 0)

            def act_first(j, last):
                for par in range(2):
                    c = 2 * j + par
                    for m, rows in enumerate(QKP):
                        act.wait_ge(qk_out[m], 16 * len(QK_RUNS[m]) * c)
                        act.wait_ge(qk_ready, 5 * c + m + 1)
                        nc.scalar.activation(qk_st[0:rows, m, 0, :], ps[0:rows, 3 + m, :], ACT.Copy).then_inc(qk_hi, 1)
                        if m == NEXT_AT and par == 0 and not last:
                            standard_deviation(j + 1, j + 1)
                        if m == NEXT_AT and (par == 0 or not last):
                            hi_of_transposed(c + 1, 1 - par)
                    for t in range(CT + 1):
                        if t < CT:
                            act.wait_ge(v_ready, CT * c + t + 1)
                            nc.scalar.activation(v_part(j, par, t)(0), ps[:, 3 + t, 0:D].rearrange("p (h d) -> p h d", h=H),
                                                 ACT.Copy).then_inc(v_hi, 1)
                        if t > 0:
                            act.wait_ge(v_evac, CT * c + t + V_CREDIT)
                            nc.scalar.activation(v_part(j, par, t - 1)(1), v_res[:, (t - 1) % 2, :].rearrange("p (h d) -> p h d", h=H),
                                                 ACT.Copy).then_inc(v_mid, 1)

            with act.Fori(0, B - 1) as j:
                act_first(j, False)
            act_first(B - 1, True)
            for b in range(B):
                for i in range(2):
                    act.wait_ge(gate_mm, 2 * b + i + 1)
                    nc.scalar.activation(gate[:, b, i, :], ps[:, GATE_BANKS[2 * b + i], 0:D], ACT.Copy).then_inc(gate_ready, 1)

            def act_head(n, r, i):
                if isinstance(n, int) and not 1 <= n <= HEADS:
                    return
                m = n - 1
                act.wait_ge(pv_ready, count(m - 2))
                for g in range(NG):
                    act.wait_ge(st_ready, NG * m + g + 1)
                    nc.scalar.activation(pt[(r - 1) % 3][:, GOFF[g]:GOFF[g] + GW[g]],
                                         slot_of(i - 1, g)[:, 0:GW[g]], ACT.Exp, scale=SCALE).then_inc(exp_done, 1)

            for n in range(FIRST):
                act_head(n, n % 3, n)
            with act.Fori(0, (HEADS - FIRST) // LOOPED) as j:
                for i in range(LOOPED):
                    act_head(LOOPED * j + FIRST + i, (FIRST + i) % 3, FIRST + i)
            act_head(HEADS, HEADS % 3, HEADS)

            def context_rows(j, par):
                for t in range(CT):
                    row = ctx_sb[:, CT * par + t, bass.ds(j, 1), :]
                    nc.scalar.activation(xn[:, par, t:t + 1, 0:D], row, ACT.Copy).then_inc(xn_ready, 1)
                    nc.scalar.activation(xn[:, par, t, D:XC].rearrange("p (e c) -> p e c", e=2),
                                         row[:, :, FULL * P:D].to_broadcast([P, 2, REM]), ACT.Copy).then_inc(xn_ready, 1)

            act.wait_ge(st_ready, NG * HEADS)
            round_weight(w1_in, 6 * 16, w1_hi, w1_h, w1_r, raw1, F, RB)
            act.wait_ge(pv_ready, HEADS - 2)
            for j in range(B):
                act.wait_ge(ctx_ready, H * (j + 1))
                act.wait_ge(t_ready, 3 * 2 * (B + j))
                for par in range(2):
                    context_rows(j, par)
                if j == B - 1:
                    act.wait_ge(w2_in, 3 * 16)
                    act.wait_ge(pv_ready, HEADS)
                    nc.scalar.activation(w2_h[:, :, :], raw2[:, :, :], ACT.Copy).then_inc(w2_hi, 1)
                    nc.scalar.activation(w2_r[RR:RB, :], raw2b[RR:RB, :], ACT.Copy).then_inc(w2_hi, 1)
                for par in range(2):
                    hi_of_transposed(2 * B + 2 * j + par, par, from_psum=True)
            standard_deviation(B, 0)
            hi_of_transposed(4 * B, 0)

            def act_mlp(j, last):
                for par in range(2):
                    c = 2 * j + par
                    for m in range(MF):
                        act.wait_ge(w1_ready, MF * c + m + 1)
                        act.wait_ge(hl_ready, MF * c + m - 3 + 1 + HS_CREDIT)
                        nc.scalar.activation(hs[:, m % 3, :], ps[:, 3 + m % 3, :], ACT.Silu).then_inc(h_ready, 1)
                    if par == 0 or not last:
                        hi_of_transposed(4 * B + c + 1, 1 - par)
                    if par == 0 and not last:
                        standard_deviation(B + j + 1, j + 1)

            with act.Fori(0, B - 1) as j:
                act_mlp(j, False)
            act_mlp(B - 1, True)

        @block.vector
        def _(dve):
            for signal, credit in ((y_ready, Y_CREDIT), (xl_ready, XL_CREDIT), (xt_used, XT_CREDIT), (v_evac, V_CREDIT),
                                   (v_split, VS_CREDIT), (res1_ready, WP_CREDIT), (x2_ready, RES_CREDIT),
                                   (x3_ready, RES_CREDIT), (h_ready, H_CREDIT), (hl_ready, HS_CREDIT), (res2_ready, W2_CREDIT)):
                dve.sem_inc(signal, credit)
            nc.vector.memset(sc_t[:], 1.0).then_inc(cond_rows, 1)
            nc.vector.memset(minus1[:].bitcast(f32), -1.0)
            nc.vector.memset(xr[RR:RB, :, :].bitcast(f32), -1.0).then_inc(cond_rows, 1)
            nc.vector.memset(ones[:].bitcast(f32), 1.0).then_inc(ones_ready, 1)
            nc.vector.memset(v_sb[:, :, :, HD:HD + 1], 1.0)
            for i in (1, 2):
                last = nc.vector.memset(v_sb[:, :, :, i * VP + HD:(i + 1) * VP], 0.0)
            last.then_inc(v_split, 1)

            def row_statistics(tile):
                nc.vector.bn_stats(stats[:, bass.ds(tile, 1), :].rearrange("p a c -> p (a c)"),
                                   x_sb[:, bass.ds(tile, 1), :].rearrange("p a c -> p (a c)")).then_inc(ln_step, 1)

            def variances(g, j):
                base = LN_STEPS * g + TQ
                dve.wait_ge(ln_step, base)
                rows = bass.ds(TQ * j, TQ)
                tt = nc.vector.tensor_tensor
                tt(lnv[:, 0, rows], stats[:, rows, 1], stats[:, rows, 4], ALU.add).then_inc(ln_step, 1)
                tt(lnv[:, 1, rows], stats[:, rows, 1], stats[:, rows, 4], ALU.subtract).then_inc(ln_step, 1)
                tt(lnv[:, 2, rows], stats[:, rows, 2], stats[:, rows, 5], ALU.add).then_inc(ln_step, 1)
                dve.wait_ge(ln_step, base + 3)
                nc.vector.tensor_scalar(lnv[:, 0, rows], lnv[:, 0, rows], 0.5, None, ALU.mult).then_inc(ln_step, 1)
                tt(lnv[:, 1, rows], lnv[:, 1, rows], lnv[:, 1, rows], ALU.mult).then_inc(ln_step, 1)
                nc.vector.tensor_scalar(lnv[:, 2, rows], lnv[:, 2, rows], 1.0 / D, EPS, ALU.mult, ALU.add).then_inc(ln_step, 1)
                dve.wait_ge(ln_step, base + 6)
                nc.vector.scalar_tensor_tensor(lnv[:, 3, rows], lnv[:, 1, rows], 0.25, lnv[:, 2, rows], ALU.mult, ALU.add).then_inc(ln_step, 1)

            def inverse_deviations(g, j):
                dve.wait_ge(std_ready, g + 1)
                rows = bass.ds(TQ * j, TQ)
                nc.vector.reciprocal(lnv[:, 5, rows], lnv[:, 4, rows]).then_inc(ln_step, 1)
                dve.wait_ge(ln_step, LN_STEPS * (g + 1))

            def normalized_rows(j, par):
                for t in range(CT):
                    tile = TQ * j + CT * par + t
                    mean, rstd = lnv[:, 0, bass.ds(tile, 1)], lnv[:, 5, bass.ds(tile, 1)]
                    nc.vector.tensor_scalar(xn[:, par, t:t + 1, 0:D], x_sb[:, bass.ds(tile, 1), :], mean, rstd,
                                            ALU.subtract, ALU.mult).then_inc(xn_ready, 1)
                    nc.vector.tensor_scalar(xn[:, par, t, D:XC].rearrange("p (e c) -> p e c", e=2),
                                            x_sb[:, bass.ds(tile, 1), FULL * P:D].to_broadcast([P, 2, REM]), mean, rstd,
                                            ALU.subtract, ALU.mult).then_inc(xn_ready, 1)

            def transposed(cc, ci, par, kind):
                for k in range(3):
                    rows = slice(0, P) if k < FULL else slice(0, RR)
                    dve.wait_ge(t_ready, 3 * cc + k + 1)
                    dve.wait_ge(xl_ready, 3 * (ci - 2) + k + 1 + XL_CREDIT)
                    nc.vector.tensor_scalar(y[rows, par, k, :], ps[rows, k, :], mod_now[rows, k, kind + 1:kind + 2],
                                            mod_now[rows, k, kind:kind + 1], ALU.mult, ALU.add).then_inc(y_ready, 1)

            def lo_of_first(cc, ci, par):
                for k in range(3):
                    dve.wait_ge(xh_ready, 3 * cc + k + 1)
                    rows = slice(0, P) if k < FULL else slice(2 * REM, RR)
                    dst, hi = (xl[:, par, k, :], xh[:, par, k, :]) if k < FULL else (xr[rows, par, :], xr[rows, par, :])
                    nc.vector.tensor_tensor(dst, y[rows, par, k, :], hi.bitcast(f32), ALU.subtract).then_inc(xl_ready, 1)

            def modulation_of(j, kind, value):
                for rows, ks in ((slice(0, P), slice(0, FULL)), (slice(0, RR), slice(FULL, 3))):
                    nc.vector.tensor_copy(mod_now[rows, ks, kind:kind + 2],
                                          modv[rows, bass.ds(j, 1), ks, kind:kind + 2].rearrange("p a k g -> p (a k) g")).then_inc(mod_copied, 1)
                dve.wait_ge(mod_copied, value)

            def split_rest(hi_done, split, dst_r, src):
                dve.wait_ge(hi_done, FULL + 1)
                nc.vector.tensor_tensor(dst_r[REM:2 * REM, :], src[REM:2 * REM, :], dst_r[REM:2 * REM, :].bitcast(f32),
                                        ALU.subtract).then_inc(split, 1)

            def bias_rows(hi_done, value, dst_r, src):
                dve.wait_ge(hi_done, value)
                nc.vector.scalar_tensor_tensor(dst_r[RR:RB, :], dst_r[RR:RB, :].bitcast(f32), ident[RR:RB, RR + 1:RR + 2],
                                               src[RR:RB, ...], ALU.mult, ALU.subtract).then_inc(bias_split, 1)

            def modulations(first, bank, ready, signal):
                dve.wait_ge(ready, 1)
                mod_ps = ps[:, bank, 0:12 * B].rearrange("p (k g b) -> p k g b", k=3, g=4)
                for b in range(B):
                    for rows, ks in ((slice(0, P), slice(0, FULL)), (slice(0, RR), slice(FULL, 3))):
                        nc.vector.tensor_copy(modv[rows, b, ks, first], mod_ps[rows, ks, first, b]).then_inc(signal, 1)
                        nc.vector.tensor_scalar(modv[rows, b, ks, first + 1], mod_ps[rows, ks, first + 1, b], 1.0, None,
                                                ALU.add).then_inc(signal, 1)

            for t in range(TQ):
                dve.wait_ge(x_in[t // CT], 16)
                row_statistics(t)
            variances(0, 0)
            dve.wait_ge(silu_c, 1)
            dve.wait_ge(cond_rows, 2)
            for k in range(NK):
                rows = KC + 1 if k == 0 else KC
                nc.vector.tensor_copy(sc_b[0:rows, k, :, :], sc_t[0:rows, k, :].unsqueeze(2).to_broadcast([rows, B, P])).then_inc(silu_c, 1)
            inverse_deviations(0, 0)
            normalized_rows(0, 0)
            modulations(0, MOD_BANK, mod_mm, mod_ready)
            dve.wait_ge(mod_ready, 4 * B)
            modulation_of(0, 0, 2)
            split_rest(wqkv_hi, wqkv_rest, wqkv_r, raw[:, FULL, 0:3 * D])
            transposed(0, 0, 0, 0)
            lo_of_first(0, 0, 0)
            normalized_rows(0, 1)
            split_rest(wp_hi, wp_rest, wp_r, wp_stage[:, FULL, :])
            bias_rows(wp_hi, FULL + 1, wp_r, wp_stage[:, FULL, :])

            def dve_first(j, last):
                for par in range(2):
                    c = 2 * j + par
                    if par == 0 and not last:
                        for tokens_in in x_in[TQ // CT:]:
                            dve.wait_ge(tokens_in, 16)
                        for t in range(TQ):
                            row_statistics(TQ * (j + 1) + t)
                        variances(j + 1, j + 1)
                    for m, rows in enumerate(QKP):
                        dve.wait_ge(qk_hi, 5 * c + m + 1)
                        nc.vector.tensor_tensor(qk_st[0:rows, m, 1, :], ps[0:rows, 3 + m, :], qk_st[0:rows, m, 0, :].bitcast(f32),
                                                ALU.subtract).then_inc(qk_evac, 1)
                        if m == NEXT_AT and par == 1 and not last:
                            modulation_of(j + 1, 0, 2 * (j + 2))
                        if m == NEXT_AT and (par == 0 or not last):
                            transposed(c + 1, c + 1, 1 - par, 0)
                    if par == 0 and not last:
                        inverse_deviations(j + 1, j + 1)
                    for t in range(CT):
                        dve.wait_ge(v_hi, CT * c + t + 1)
                        dve.wait_ge(v_split, CT * c + t - 2 + 1 + VS_CREDIT + 1)
                        nc.vector.tensor_tensor(v_res[:, t % 2, :].rearrange("p (h d) -> p h d", h=H),
                                                ps[:, 3 + t, 0:D].rearrange("p (h d) -> p h d", h=H), v_part(j, par, t)(0),
                                                ALU.subtract).then_inc(v_evac, 1)
                    if not last:
                        normalized_rows(j + 1, par)

            with dve.Fori(0, B - 1) as j:
                dve_first(j, False)
            dve_first(B - 1, True)

            dve.wait_ge(v_ready, TILES)
            dve.wait_ge(wp_split, FULL)
            dve.wait_ge(bias_split, 1)
            nc.vector.memset(mneg[:], 0.0).then_inc(ones_ready, 1)
            dve.wait_ge(ones_ready, 2)

            def split_maximum(n, r):
                dve.wait_ge(mt_ready, n + 1)
                nc.vector.tensor_copy(m_t[0:TQ, r, 0, :], slot1[0:TQ, 0:P]).then_inc(mt_hi, 1)
                dve.wait_ge(mt_hi, n + 1)
                nc.vector.tensor_tensor(m_t[0:TQ, r, 1, :], slot1[0:TQ, 0:P], m_t[0:TQ, r, 0, :].bitcast(f32),
                                        ALU.subtract).then_inc(mt_used, 1)

            def vector_lo(n, r, g):
                dve.wait_ge(exp_done, NG * n + g + 1)
                lo_part(nc.vector, n, r, g).then_inc(lo_vector, 1)

            def sums(n, r):
                dve.wait_ge(pv_ready, n + 1)
                dve.wait_ge(ctx_ready, count(n - 2))
                nc.vector.tensor_reduce(csum[:, r, :, :], pv.rearrange("p i (e d) -> p i d e", e=3), axis=AX.X,
                                        op=ALU.add).then_inc(pv_used, 1)
                dve.wait_ge(pv_used, n + 1)
                nc.vector.reciprocal(rden[:, r, :], csum[:, r, :, HD]).then_inc(rden_ready, 1)

            def dve_head(n, r):
                fixed = isinstance(n, int)
                for s, i in enumerate(ORDER):
                    if s == 0 and (not fixed or 1 <= n <= HEADS):
                        split_maximum(n - 1, (r - 1) % 3)
                    if not fixed or n < HEADS:
                        dve.wait_ge(max_ready, TQ * n + s + 1)
                        src = (slot2 if s % 2 == 0 else slot1)[:, 0:(i + 1) * P]
                        nc.vector.tensor_reduce(mneg[:, r, i:i + 1], src, axis=AX.X, op=ALU.max, negate=True).then_inc(max_used, 1)
                    if s in LO_VECTOR_AT and (not fixed or 2 <= n <= HEADS + 1):
                        vector_lo(n - 2, (r - 2) % 3, LO_VECTOR_AT[s])
                        for g in LAST_LOS[0][1:] if fixed and n == HEADS + 1 else ():
                            vector_lo(n - 2, (r - 2) % 3, g)
                    if s == SUMS_AT and (not fixed or 3 <= n <= HEADS + 2):
                        sums(n - 3, r)

            for n in range(FIRST):
                dve_head(n, n % 3)
                if n == 0:
                    modulations(2, MOD2_BANK, mod2_mm, mod2_ready)
            with dve.Fori(0, (HEADS - FIRST) // LOOPED) as j:
                for i in range(LOOPED):
                    dve_head(LOOPED * j + FIRST + i, (FIRST + i) % 3)
            def context_lo(cc, par):
                for k in range(3):
                    dve.wait_ge(xh_ready, 3 * cc + k + 1)
                    if k < FULL:
                        nc.vector.tensor_tensor(xl[:, par, k, :], ps[:, k, :], xh[:, par, k, :].bitcast(f32),
                                                ALU.subtract).then_inc(y_ready, 1)
                    else:
                        rows = slice(2 * REM, RR)
                        nc.vector.tensor_tensor(xr[rows, par, :], ps[rows, k, :], xr[rows, par, :].bitcast(f32),
                                                ALU.subtract).then_inc(y_ready, 1)

            for n in range(HEADS, HEADS + 2):
                dve_head(n, n % 3)

            split_rest(w1_hi, w1_rest, w1_r, raw1[:, FULL, :])
            bias_rows(w1_hi, FULL + 1, w1_r, raw1[:, FULL, :])
            dve_head(HEADS + 2, (HEADS + 2) % 3)
            for par in range(2):
                context_lo(2 * B + par, par)

            def tile_statistics_of(t, j):
                dve.wait_ge(x2_ready, TQ * j + t + 1 + RES_CREDIT)
                row_statistics(TQ * j + t)

            def gated_context(j, par, lagging=True):
                for t in range(CT):
                    n = TQ * j + CT * par + t
                    dve.wait_ge(wp_ready, n + 1)
                    dve.wait_ge(x2_ready, n - CT + 1 + RES_CREDIT)
                    nc.vector.tensor_tensor(res[:, t:t + 1, :], ps[:, 3 + t:4 + t, 0:D],
                                            gate[:, bass.ds(j, 1), 0, :], ALU.mult).then_inc(res1_ready, 1)
                    if CT * par + t >= STATS_LAG and (par == 0 or lagging):
                        tile_statistics_of(CT * par + t - STATS_LAG, j)

            def last_statistics(j, first):
                for t in range(first, TQ):
                    tile_statistics_of(t, j)

            with dve.Fori(0, B - 1) as j:
                for par in range(2):
                    gated_context(j, par)
                context_lo(2 * B + 2 * (j + 1), 0)
                last_statistics(j, TQ - STATS_LAG)
                context_lo(2 * B + 2 * (j + 1) + 1, 1)
            variances(B, 0)
            inverse_deviations(B, 0)
            modulation_of(0, 2, 2 * B + 2)
            normalized_rows(0, 0)
            gated_context(B - 1, 0)
            transposed(4 * B, 2 * B, 0, 2)
            lo_of_first(4 * B, 2 * B, 0)
            gated_context(B - 1, 1, lagging=False)
            bias_rows(w2_hi, 2, w2_r, raw2b)
            normalized_rows(0, 1)
            last_statistics(B - 1, CT - STATS_LAG)

            def dve_mlp(j, last):
                for par in range(2):
                    c = 2 * j + par
                    if par == 0 and not last:
                        variances(B + j + 1, j + 1)
                    dve.wait_ge(w2_ready, CT * c)
                    for m in range(MF):
                        dve.wait_ge(h_ready, MF * c + m + 1 + H_CREDIT)
                        nc.vector.tensor_copy(h_h[:, m, :], hs[:, m % 3, :]).then_inc(hh_ready, 1)
                    if par == 1 and not last:
                        modulation_of(j + 1, 2, 2 * B + 2 * (j + 2))
                    if par == 0 or not last:
                        transposed(4 * B + c + 1, 2 * B + c + 1, 1 - par, 2)
                    for t in range(CT):
                        n = CT * c + t
                        dve.wait_ge(w2_ready, n + 1)
                        dve.wait_ge(x3_ready, n - CT + 1 + RES_CREDIT)
                        nc.vector.tensor_tensor(res[:, t:t + 1, :], ps[:, 6 + t % 2:7 + t % 2, 0:D],
                                                gate[:, bass.ds(j, 1), 1, :], ALU.mult).then_inc(res2_ready, 1)
                    if not last:
                        if par == 0:
                            inverse_deviations(B + j + 1, j + 1)
                        normalized_rows(j + 1, par)

            with dve.Fori(0, B - 1) as j:
                dve_mlp(j, False)
            dve_mlp(B - 1, True)

        @block.tensor
        def _(pe):
            mm = nc.tensor.matmul

            def modulation_products(ks, gs, bank):
                for k in ks:
                    for g in gs:
                        group = (0, 1, 3, 4)[g]
                        at = (k * 4 + g) * B
                        for p0, cols in ([(0, P)] if k < FULL else [(i * REM, REM) for i in range(3)]):
                            for kk in range(NK):
                                rows = KC + 1 if kk == 0 else KC
                                last = mm(ps[p0:p0 + cols, bank, at:at + B],
                                          wa_sb[0:rows, kk, group * D + k * P:group * D + k * P + cols],
                                          sc_t[0:rows, kk, :], start=kk == 0, stop=kk == NK - 1)
                return last

            def gate_products(b, i):
                for kk in range(NK):
                    rows = KC + 1 if kk == 0 else KC
                    group = (2, 5)[i]
                    last = mm(ps[:, GATE_BANKS[2 * b + i], 0:D], sc_b[0:rows, kk, b, :], wa_sb[0:rows, kk, group * D:(group + 1) * D],
                              start=kk == 0, stop=kk == NK - 1)
                return last

            pe.wait_ge(wa_in, 32)
            pe.wait_ge(silu_c, 1)
            pe.wait_ge(cond_rows, 2)
            modulation_products(range(3), (0, 1), MOD_BANK).then_inc(mod_mm, 1)

            def transposes(cc, par):
                pe.wait_ge(xn_ready, 2 * CT * (cc + 1))
                for k in range(3):
                    cols = slice(k * P, (k + 1) * P) if k < FULL else slice(FULL * P, XC)
                    rows = P if k < FULL else RR
                    pe.wait_ge(y_ready, 3 * (cc - 1) + k + 1 + Y_CREDIT)
                    for t in range(CT):
                        last = nc.tensor.transpose(ps[0:rows, k, t * P:(t + 1) * P], xn[:, par, t, cols], ident[:])
                    last.then_inc(t_ready, 1)

            def products(out_ap, terms):
                for i, (lhs, rhs) in enumerate(terms):
                    last = mm(out_ap, lhs, rhs, start=i == 0, stop=i == len(terms) - 1)
                return last

            def weights_first(out_ap, wh, wl, wr, cols, par, rows):
                return products(out_ap, [(w, a) for k in range(FULL) for w, a in (
                    (wh[:, k, cols], xh[:, par, k, :]), (wl[:, k, cols], xh[:, par, k, :]), (wh[:, k, cols], xl[:, par, k, :]))]
                    + [(wr[0:rows, cols], xr[0:rows, par, :])])

            def tokens_first(out_ap, wh, wl, wr, cols, par, t, rows):
                tok = slice(t * P, (t + 1) * P)
                return products(out_ap, [(a, w) for k in range(FULL) for a, w in (
                    (xh[:, par, k, tok], wh[:, k, cols]), (xh[:, par, k, tok], wl[:, k, cols]), (xl[:, par, k, tok], wh[:, k, cols]))]
                    + [(xr[0:rows, par, tok], wr[0:rows, cols])])

            pe.wait_ge(consts_made, 1)
            transposes(0, 0)
            pe.wait_ge(mod_ready, 4 * B)
            pe.wait_ge(wqkv_split, FULL)
            pe.wait_ge(wqkv_rest, 1)

            def pe_first(j, last):
                for par in range(2):
                    c = 2 * j + par
                    pe.wait_ge(xl_ready, 3 * (c + 1) + XL_CREDIT)
                    for m, rows in enumerate(QKP):
                        if m < CT:
                            pe.wait_ge(v_evac, CT * (c - 1) + m + 1 + V_CREDIT)
                        else:
                            pe.wait_ge(qk_evac, 5 * c)
                        weights_first(ps[:, 3 + m, :], wqkv_h, wqkv_l, wqkv_r, slice(m * P, (m + 1) * P), par, RR).then_inc(qk_ready, 1)
                        if m == NEXT_AT and (par == 0 or not last):
                            transposes(c + 1, 1 - par)
                    for t in range(CT):
                        pe.wait_ge(qk_evac, 5 * c + t + 1)
                        tokens_first(ps[:, 3 + t, 0:D], wqkv_h, wqkv_l, wqkv_r, slice(2 * D, 3 * D), par, t, RR).then_inc(v_ready, 1)
                    pe.wait_ge(v_ready, CT * (c + 1))
                    pe.sem_inc(xt_used, 1)

            with pe.Fori(0, B - 1) as j:
                pe_first(j, False)
            pe_first(B - 1, True)

            pe.wait_ge(y_ready, 3 * 2 * B + Y_CREDIT)
            pe.wait_ge(qk_evac, 5 * 2 * B)
            pe.wait_ge(wa_rest_in, 16)
            pe.wait_ge(silu_c, 1 + NK)
            for b in range(B):
                for i in range(2):
                    gate_products(b, i).then_inc(gate_mm, 1)
            pe.wait_ge(gate_ready, 2 * B)

            def pe_head(n, r, k3, place_of):
                fixed = isinstance(n, int)
                q, k = stack(q_st, r), stack(k_st, r)
                if fixed and n == WARM_AT:
                    warm = v_sb[:, 0, :, :].rearrange("p k c -> p (k c)")
                    pe.wait_ge(exp_done, NG * (n - 1) - 1)
                    for _ in range(8):
                        mm(slot_of(n - 1, 0)[:, 0:TQ * 3 * VP], ident_b[:], warm, start=True, stop=True)
                scores, maxima = not fixed or n < HEADS, not fixed or 1 <= n <= HEADS
                values = not fixed or 3 <= n <= HEADS + 2
                for s, i in enumerate(ORDER):
                    if s == 0 and maxima:
                        pe.wait_ge(max_used, TQ * n)
                        nc.tensor.transpose(slot1[:, 0:P], mneg[:, (r - 1) % 3, :], ident[:]).then_inc(mt_ready, 1)
                    if scores:
                        if s == 0:
                            pe.wait_ge(stacks_in[r], 6 * 16 * (k3 + 1))
                        pe.wait_ge(max_used, count(TQ * n + s - 1))
                        if s == 1:
                            pe.wait_ge(mt_used, n)
                        slot = slot2 if s % 2 == 0 else slot1
                        for c0 in range(0, (i + 1) * P, CHUNK):
                            c1 = min(c0 + CHUNK, (i + 1) * P)
                            mm(slot[:, c0:c1], q[0:SR, i * P:(i + 1) * P], k[0:SR, c0:c1], start=True, stop=c1 < (i + 1) * P)
                        mm(slot[:, i * P:(i + 1) * P], ident_b[:], mask[:], start=False, stop=True).then_inc(max_ready, 1)
                    if fixed and n == 0 and s == 0:
                        pe.wait_ge(v_evac, TILES + V_CREDIT)
                    if fixed and n == 0 and s < 6:
                        last = modulation_products((s // 2,), (2 + s % 2,), MOD2_BANK)
                        if s == 5:
                            last.then_inc(mod2_mm, 1)
                    if fixed and n == 1 and s == 0:
                        pe.wait_ge(mod2_ready, 4 * B)
                        pe.wait_ge(ones_in, 3 * 16)
                        pe.wait_ge(v_split, TILES + 1 + VS_CREDIT)
                    if values:
                        for tile in VALUES_AT[s]:
                            weighted_values(n - 3, r, tile)
                    if s == TQ - 1 and (not fixed or 2 <= n <= HEADS + 1):
                        for tile in EARLY_VALUES:
                            weighted_values(n - 2, (r - 2) % 3, tile)
                    for g in SCORES_T_AT[s] if maxima else ():
                        transposed_scores(n - 1, (r - 1) % 3, k3 if r else k3 - 1, g, place_of - 1)

            def transposed_scores(n, r, k3, g, place_of):
                q, k = stack(q_st, r), stack(k_st, r)
                slot = slot_of(place_of, g)
                if g == 0:
                    pe.wait_ge(m_rows[r], 2 * 16 * (k3 + 1))
                pe.wait_ge(exp_done, count(NG * n + g - 1))
                for kt in GROUPS[g]:
                    at = KOFF[kt] - GOFF[g]
                    c0 = 0
                    while c0 < L - P * kt:
                        c1 = min((at + c0) // CHUNK * CHUNK + CHUNK - at, L - P * kt)
                        mm(slot[:, at + c0:at + c1], k[:, kt * P:(kt + 1) * P], q[:, kt * P + c0:kt * P + c1],
                           start=(at + c0) % CHUNK == 0, stop=c0 > 0, skip_group_check=True)
                        c0 = c1
                    last = mm(slot[:, at:at + P], ident_b[:], mask_t[:], start=False, stop=True, skip_group_check=True)
                last.then_inc(st_ready, 1)

            def weighted_values(n, r, i):
                if i == 0:
                    pe.wait_ge(pv_used, n)
                own, others = LAST_LOS if isinstance(n, int) and n == HEADS - 1 else (VECTOR_LOS, POOL_LOS)
                for signal, groups, each in ((lo_vector, own, len(VECTOR_LOS)), (lo_pool, others, len(POOL_LOS))):
                    done = max([groups.index(GROUP_OF[kt]) + 1 for kt in range(i + 1) if GROUP_OF[kt] in groups], default=0)
                    if done:
                        pe.wait_ge(signal, each * n + done)
                for kt in range(i + 1):
                    cols = slice(KOFF[kt] + (i - kt) * P, KOFF[kt] + (i - kt + 1) * P)
                    v = v_sb[:, bass.ds(n, 1), kt, :]
                    hi = pt[r][:, cols].bitcast(bf16).rearrange("p (n e) -> p n e", e=2)[:, :, 1]
                    mm(pv[:, i:i + 1, :], hi, v, start=kt == 0, stop=False)
                    last = mm(pv[:, i:i + 1, :], pt_lo[r][:, cols], v, start=False, stop=kt == i)
                if i == TQ - 1:
                    last.then_inc(pv_ready, 1)

            for n in range(FIRST):
                pe_head(n, n % 3, n // 3, n)
            with pe.Fori(0, (HEADS - FIRST) // LOOPED) as j:
                for i in range(LOOPED):
                    pe_head(LOOPED * j + FIRST + i, (FIRST + i) % 3, LOOPED // 3 * j + (FIRST + i) // 3, FIRST + i)
            for n in range(HEADS, HEADS + 2):
                pe_head(n, n % 3, n // 3, n)

            pe_head(HEADS + 2, (HEADS + 2) % 3, (HEADS + 2) // 3, HEADS + 2)
            pe.wait_ge(mt_used, HEADS)
            for par in range(2):
                transposes(2 * B + par, par)
            pe.wait_ge(exp_done, NG * HEADS)
            pe.wait_ge(wp_split, FULL)
            pe.wait_ge(wp_rest, 1)
            pe.wait_ge(bias_split, 1)

            def projection(j, par):
                c = 2 * j + par
                pe.wait_ge(y_ready, 3 * (2 * B + c + 1) + Y_CREDIT)
                for t in range(CT):
                    pe.wait_ge(res1_ready, CT * (c - 1) + t + 1 + WP_CREDIT)
                    tokens_first(ps[:, 3 + t, 0:D], wp_h, wp_l, wp_r, slice(0, D), par, t, RB).then_inc(wp_ready, 1)
                pe.wait_ge(wp_ready, CT * (c + 1))
                pe.sem_inc(xt_used, 1)

            with pe.Fori(0, B - 1) as j:
                for par in range(2):
                    projection(j, par)
                for par in range(2):
                    transposes(2 * B + 2 * (j + 1) + par, par)
            projection(B - 1, 0)
            transposes(4 * B, 0)
            projection(B - 1, 1)

            pe.wait_ge(w1_split, FULL)
            pe.wait_ge(w1_rest, 1)
            pe.wait_ge(bias_split, 2)

            def pe_mlp(j, last):
                for par in range(2):
                    c = 2 * j + par
                    pe.wait_ge(xl_ready, 3 * (2 * B + c + 1) + XL_CREDIT)
                    for m in range(MF):
                        if m < 3:
                            pe.wait_ge(res1_ready, TILES - CT + m + 1 + WP_CREDIT)
                        pe.wait_ge(h_ready, MF * c + m - 3 + 1 + H_CREDIT)
                        weights_first(ps[:, 3 + m % 3, :], w1_h, w1_l, w1_r, slice(m * P, (m + 1) * P), par, RB).then_inc(w1_ready, 1)
                    pe.wait_ge(w1_ready, MF * (c + 1))
                    pe.sem_inc(xt_used, 1)
                    if par == 0 or not last:
                        transposes(4 * B + c + 1, 1 - par)
                    for t in range(CT):
                        n = CT * c + t
                        tok = slice(t * P, (t + 1) * P)
                        pe.wait_ge(res2_ready, n - 2 + 1 + W2_CREDIT)
                        pe.wait_ge(res1_ready, TILES + WP_CREDIT)
                        pe.wait_ge(pv_used, HEADS)
                        pe.wait_ge(w2_split, 1)
                        pe.wait_ge(bias_split, 3)
                        for m in range(MF):
                            if t == 0:
                                pe.wait_ge(hl_ready, MF * c + m + 1 + HS_CREDIT)
                            for i, (a, w) in enumerate(((h_h, w2_h), (h_h, w2_l), (h_l, w2_h))):
                                mm(ps[:, 6 + t % 2, 0:D], a[:, m, tok], w[:, m, :], start=m == 0 and i == 0, stop=False)
                        mm(ps[:, 6 + t % 2, 0:D], minus1[RR:RB, :], w2_r[RR:RB, :], start=False, stop=True).then_inc(w2_ready, 1)

            with pe.Fori(0, B - 1) as j:
                pe_mlp(j, False)
            pe_mlp(B - 1, True)


_INPUTS = ["x", "cond_1152", "L0_cond_Wq", "L0_cond_Wk", "L0_cond_Wv", "L0_cond_Wp", "L0_cond_bp", "L0_cond_W1",
           "L0_cond_b1", "L0_cond_W2", "L0_cond_b2", "L0_cond_Wa", "L0_cond_ba"]


def kernel(**inputs):
    import concourse.bacc as bacc
    from concourse.bass_utils import run_bass_kernel_spmd

    nc = bacc.Bacc("TRN2", target_bir_lowering=False, num_devices=1)
    arrays, args = {}, []
    for name in _INPUTS:
        a = np.ascontiguousarray(inputs[name])
        arrays[f"in_{name}"] = a
        args.append(nc.dram_tensor(f"in_{name}", a.shape, mybir.dt.from_np(a.dtype), kind="ExternalInput").ap())
    out = nc.dram_tensor("out", arrays["in_x"].shape, mybir.dt.float32, kind="ExternalOutput").ap()
    conditioned_transformer_block(nc, *args, out)
    r = run_bass_kernel_spmd(nc, [arrays], core_ids=[0])
    return r.results[0]["out"]
```
